# Optimizing a Trainium2 kernel written in Bass

```python
import numpy as np
import jax
import jax.numpy as jnp

def _softmax(x, axis=-1):
    return jax.nn.softmax(x, axis=axis)

def _gelu(x):
    return jax.nn.gelu(x, approximate=True)

def _silu(x):
    return jax.nn.silu(x)

def _sigmoid(x):
    return jax.nn.sigmoid(x)

def _layernorm(x, axis=-1, eps=1e-05):
    m = jnp.mean(x, axis=axis, keepdims=True)
    v = jnp.var(x, axis=axis, keepdims=True)
    return (x - m) / jnp.sqrt(v + eps)

def _scatter_add(tgt, idx, src, axis=0):
    return tgt.at[idx].add(src)

def _segment_sum(src, seg, n):
    return jax.ops.segment_sum(src, seg, n)
kernel_name = 'mk_flamingo_gated_d1_seqx_r2_9a48d0'

def setup_inputs(seed: int=0):
    np.random.seed(seed)
    _w = jnp.asarray

    def _rec_inputs():
        import jax
        import jax.numpy as jnp
        _rk = jax.random.key(seed)
        x = -0.0003929 + 0.9999 * jax.random.normal(jax.random.fold_in(_rk, 1), (16, 224, 512), jnp.float32)
        _lenS = 224 - jax.random.randint(jax.random.fold_in(_rk, 7), (16,), 0, max(1, 224 // 4) + 1, jnp.int32)
        _lenS2 = 750 - jax.random.randint(jax.random.fold_in(_rk, 8), (16,), 0, max(1, 750 // 4) + 1, jnp.int32)
        _ctx_1024P = jax.random.normal(jax.random.fold_in(_rk, 11), (16, 16, 512), jnp.float32)
        _ctx_1024c = jax.random.dirichlet(jax.random.fold_in(_rk, 511), 0.3 * jnp.ones((16,), jnp.float32), (16, 750))
        _ctx_1024t = jnp.einsum('bsk,bkd->bsd', _ctx_1024c, _ctx_1024P)
        _ctx_1024t = _ctx_1024t * jax.lax.rsqrt(jnp.mean(jnp.square(_ctx_1024t)) + 1e-12) * 0.953939
        ctx_1024 = -3.05549e-07 + 0.0199987 * (_ctx_1024t + 0.3 * jax.random.normal(jax.random.fold_in(_rk, 611), (16, 750, 512), jnp.float32))
        _g = jax.random.normal(jax.random.fold_in(_rk, 9001), (2, 1), jnp.float32)
        _g = jnp.sign(_g) * jnp.maximum(jnp.abs(_g), 1.0) + (_g == 0) * 1.0
        g_xattn = _g[0]
        g_ffn = _g[1]
        return (x, ctx_1024, g_xattn, g_ffn)
    x, ctx_1024, g_xattn, g_ffn = _rec_inputs()

    def _L0_xattn_setup():
        import jax, jax.numpy as jnp
        import numpy as np
        E, T, H, F = (8, 1024, 512, 2048)
        key = jax.random.key(seed)
        k1, k2, k3 = jax.random.split(key, 3)
        x = jax.random.normal(k1, (E, T, H), dtype=jnp.float32)
        w1 = jax.random.normal(k2, (E, F, H), dtype=jnp.float32) * 0.02
        w2 = jax.random.normal(k3, (E, F, H), dtype=jnp.float32) * 0.02
        return {'x': x, 'w1': w1, 'w2': w2}
    _L0_xattn_all = _L0_xattn_setup()
    _L0_xattn_in = {k: v for k, v in _L0_xattn_all.items() if k in ()}
    del _L0_xattn_all

    def _L0_ffn_setup():
        import jax, jax.numpy as jnp
        import numpy as np
        TOP_K = 2
        key = jax.random.key(seed)
        k_x, k_g, k_w1, k_w2, k_w3 = jax.random.split(key, 5)
        B, S, D, H, E = (2, 256, 512, 256, 8)
        x = jax.random.normal(k_x, (B, S, D), dtype=jnp.float32)
        gate_w = jax.random.normal(k_g, (D, E), dtype=jnp.float32) * D ** (-0.5)
        w1 = jax.random.normal(k_w1, (E, D, H), dtype=jnp.float32) * 0.02
        w2 = jax.random.normal(k_w2, (E, H, D), dtype=jnp.float32) * 0.02
        w3 = jax.random.normal(k_w3, (E, D, H), dtype=jnp.float32) * 0.02
        return {'x': x, 'gate_w': gate_w, 'w1': w1, 'w2': w2, 'w3': w3}
    _L0_ffn_all = _L0_ffn_setup()
    _L0_ffn_in = {k: v for k, v in _L0_ffn_all.items() if k in ('gate_w', 'w1', 'w2', 'w3')}
    del _L0_ffn_all
    return {'x': x, 'ctx_1024': ctx_1024, 'g_xattn': g_xattn, 'g_ffn': g_ffn, 'L0_ffn_gate_w': _L0_ffn_in['gate_w'], 'L0_ffn_w1': _L0_ffn_in['w1'], 'L0_ffn_w2': _L0_ffn_in['w2'], 'L0_ffn_w3': _L0_ffn_in['w3']}

def reference(x, ctx_1024, g_xattn, g_ffn, L0_ffn_gate_w, L0_ffn_w1, L0_ffn_w2, L0_ffn_w3):
    import jax
    import jax.numpy as jnp

    def _L0_xattn_ref(x, w1, w2):
        import jax, jax.numpy as jnp
        import numpy as np
        E, T, H, F = (8, 1024, 512, 2048)
        h = jnp.einsum('eth,efh->etf', x, w1)
        a = jax.nn.gelu(h, approximate=True)
        return jnp.einsum('etf,efh->eth', a, w2)

    def _L0_ffn_ref(x, gate_w, w1, w2, w3):
        import jax, jax.numpy as jnp
        import numpy as np
        TOP_K = 2
        B, S, D = x.shape
        E = gate_w.shape[1]
        xf = x.reshape(B * S, D)
        T = B * S
        logits = xf @ gate_w
        scores = jax.nn.softmax(logits, axis=-1)
        top_scores, top_idx = jax.lax.top_k(scores, TOP_K)
        scale = jnp.zeros((T, E), dtype=x.dtype).at[jnp.arange(T)[:, None], top_idx].set(top_scores)
        xs = scale.T[:, :, None] * xf[None, :, :]
        h = jax.nn.silu(jnp.einsum('etd,edh->eth', xs, w1)) * jnp.einsum('etd,edh->eth', xs, w3)
        y = jnp.einsum('eth,ehd->etd', h, w2)
        out = y.sum(axis=0)
        return out.reshape(B, S, D)
    x = x + jnp.tanh(g_xattn[0]) * _L0_xattn_ref(_layernorm(x, axis=-1), ctx_1024, ctx_1024)
    x = x + jnp.tanh(g_ffn[0]) * _L0_ffn_ref(_layernorm(x, axis=-1), L0_ffn_gate_w, L0_ffn_w1, L0_ffn_w2, L0_ffn_w3)
    return x

_drawn_inputs = setup_inputs


def setup_inputs(seed=0):
    import zlib

    import numpy as np

    out = dict(_drawn_inputs(seed))
    spreads = {}
    factors = {'L0_ffn_gate_w': 8.0, 'L0_ffn_w1': 8.0, 'L0_ffn_w2': 8.0, 'L0_ffn_w3': 8.0}
    for name, (base, spread) in spreads.items():
        noise = np.random.default_rng([zlib.crc32(name.encode()), seed]).standard_normal(out[name].shape)
        drawn = base * np.exp(spread * noise) if base else spread * noise
        out[name] = jnp.asarray(drawn.astype(out[name].dtype))
    for name, factor in factors.items():
        out[name] = (out[name] * factor).astype(out[name].dtype)
    return out
```

```python
import concourse.bass as bass
from concourse import mybir
from contextlib import ExitStack
import numpy as np

F32 = mybir.dt.float32
I32 = mybir.dt.int32
U32 = mybir.dt.uint32
ALU = mybir.AluOpType
ACT = mybir.ActivationFunctionType
AX = mybir.AxisListType

B, S, D = 16, 224, 512
C = 750
E, HID, TOPK = 8, 256, 2
T = B * S
EPS = 1e-5

P = 128
TT = S // 2
CR, NC = 125, 6
KD = D // P
KH = HID // P
EB = T // P
TRASH = E * EB
NB = (T * TOPK) // P + E - 1
AHEAD = 2
NBM = NB + AHEAD
RING = 6
assert (NB - AHEAD - 1) % RING == 0


def hold(eng, sem, value):
    eng.wait_ge(sem, value)
    eng.nop(nofuse=True)


class Seq:

    def __init__(self, eng, sem, base=0):
        self.eng, self.sem, self.base, self.n = eng, sem, base, 0

    def done(self, ins):
        self.n += 1
        return ins.then_inc(self.sem, 1)

    def settle(self):
        hold(self.eng, self.sem, self.base + self.n)


def build(nc, x, ctx, g_xattn, g_ffn, gate_w, w1, w2, w3, out):
    xf_dram = nc.dram_tensor("xf_rows", (T + P, D), F32).ap()
    table = nc.dram_tensor("route_table", ((TRASH + 1) * P, 2), I32).ap()

    st = ExitStack()
    with st:
        def sb(name, shape, dt=F32):
            return st.enter_context(nc.sbuf_tensor(name, shape, dt))

        def ps(name, shape, dt=F32):
            return st.enter_context(nc.psum_tensor(name, shape, dt))

        def sem(name):
            return st.enter_context(nc.semaphore(name))

        w13 = sb("w13", [P, E * KD * 2 * HID])
        w2s = sb("w2s", [P, E * KH * D])
        gate = sb("gate", [P, KD, E])
        ident = sb("ident", [P, P])
        lower = sb("lower", [TT, TT])
        ones = sb("ones", [TT, P])
        zeros = sb("zeros", [P, D])
        iota_e = sb("iota_e", [TT, E])
        ebase = sb("ebase", [TT, E])
        tok = sb("tok", [TT, 2])
        neg_half = sb("neg_half", [TT, 4])
        euler = sb("euler", [TT, 2 * E])
        init_i = sb("init_i", [P, TRASH + 1], I32)
        init_t = sb("init_t", [P, TRASH + 1, 2], I32)
        g_raw = sb("g_raw", [P, 2])
        g_tanh = sb("g_tanh", [P, 2])
        ctx_sb = [sb(f"ctx{u}", [CR, NC, D]) for u in range(2)]
        ctxT = [sb(f"ctxT{u}", [P, KD, C]) for u in range(2)]
        x_sb = [sb(f"x{u}", [TT, 2, D]) for u in range(2)]
        xn = sb("xn", [TT, 2, D])
        xnT = [sb(f"xnT{u}", [P, KD, S]) for u in range(2)]
        aT = sb("aT", [CR, NC, S])
        x2 = [sb(f"x2{u}", [TT, 2, D]) for u in range(2)]
        xf = [sb(f"xf{u}", [TT, 2, D]) for u in range(2)]
        xfT = sb("xfT", [P, 2, KD, TT])
        stats = sb("stats", [TT, 2, 6])
        mv1 = sb("mv1", [TT, 2, 2])
        mv2 = sb("mv2", [TT, 2, 2])
        ve = sb("ve", [TT, 4])
        rstd = sb("rstd", [TT, 4])
        lg = sb("lg", [TT, 2, E])
        mx = sb("mx", [TT, 2, 8])
        ix = sb("ix", [TT, 2, 8], U32)
        ixf = sb("ixf", [TT, 2, TOPK])
        oh = sb("oh", [TT, 2, TOPK, E])
        M = sb("M", [TT, 2, E])
        R = sb("R", [TT, 2, E])
        dl = sb("dl", [TT, 2, E])
        ex = sb("ex", [TT, 2, E])
        sm = sb("sm", [TT, 2])
        rs = sb("rs", [TT, 2])
        pos_e = sb("pos_e", [TT, 2, E])
        pos_o = sb("pos_o", [TT, 2, TOPK, E])
        pos_f = sb("pos_f", [TT, 2 * TOPK])
        pos_i = [sb(f"pos_i{u}", [TT, 2 * TOPK], I32) for u in range(2)]
        route = [sb(f"route{u}", [TT, 2, TOPK, 2], I32) for u in range(2)]
        cnt_i = sb("cnt_i", [1, E], I32)
        nblk = sb("nblk", [1, E])
        first = sb("first", [1, E + 1])
        gap = sb("gap", [1, E])
        bidx = sb("bidx", [1, NBM])
        m_e = sb("m_e", [1, NBM])
        m_r = sb("m_r", [1, NBM])
        m_t = sb("m_t", [1, NBM])
        bmap = sb("bmap", [1, 2, NBM], I32)
        meta = [sb(f"meta{n}", [P, 2], I32) for n in range(RING)]
        score = [meta[n][:, 1:2].bitcast(F32) for n in range(RING)]
        xg = [sb(f"xg{u}", [P, D]) for u in range(2)]
        xgT = [ctxT[u][:, 0, 0:KD * P] for u in range(2)]
        sg, hh, hhT = ctxT[0][:, 1, 0:HID], ctxT[1][:, 1, 0:HID], ctxT[0][:, 2, 0:KH * P]
        y_sb = [sb(f"y{u}", [P, D]) for u in range(2)]
        bank = [ps(f"bank{n}", [P, 512]) for n in range(8)]
        T_ps, H_ps, O_ps, X_ps, L_ps = bank[0:2], bank[2:4], bank[4:6], bank[6], bank[7]
        lg_ps, rk_ps = L_ps[0:TT, 0:2 * E], L_ps[0:TT, 64:64 + 2 * E]
        cnt_ps = L_ps[:, 128:128 + E]

        small_loaded = sem("small_loaded")
        consts = sem("consts")
        pool_seq = sem("pool_seq")
        dve_seq = sem("dve_seq")
        tanh_ready = sem("tanh_ready")
        table_ready = sem("table_ready")
        x_loaded = [sem(f"x_loaded{u}") for u in range(2)]
        ctx_loaded = [[sem(f"ctx_loaded{u}_{c}") for c in range(NC)] for u in range(2)]
        w_loaded = sem("w_loaded")
        ctxT_made, ctxT_ready = sem("ctxT_made"), sem("ctxT_ready")
        h_made, a_ready, attn_part = sem("h_made"), sem("a_ready"), sem("attn_part")
        xn_ready, xn_seen = sem("xn_ready"), sem("xn_seen")
        small_made, small_ready = sem("small_made"), sem("small_ready")
        x2_ready, xf_ready = sem("x2_ready"), sem("xf_ready")
        mv1_ready, mv2_ready, rstd1_ready, rstd2_ready = (sem(n) for n in ("mv1_ready", "mv2_ready", "rstd1_ready", "rstd2_ready"))
        logits_made, mask_ready, rank_made, pos_read = (sem(n) for n in ("logits_made", "mask_ready", "rank_made", "pos_read"))
        dl_ready, ex_ready = sem("dl_ready"), sem("ex_ready")
        route_ready = sem("route_ready")
        x2_stored = [sem(f"x2_stored{u}") for u in range(2)]
        xf_stored = [sem(f"xf_stored{u}") for u in range(2)]
        routed = [sem(f"routed{u}") for u in range(2)]
        counts_made, map_ready = sem("counts_made"), sem("map_ready")
        phase2 = sem("phase2")
        meta_loaded = [sem(f"meta_loaded{n}") for n in range(RING)]
        gathered = [sem(f"gathered{u}") for u in range(2)]
        xgT_made, xgT_ready = sem("xgT_made"), sem("xgT_ready")
        up_made, sg_ready, hh_ready = sem("up_made"), sem("sg_ready"), sem("hh_ready")
        hhT_made, hhT_ready = sem("hhT_made"), sem("hhT_ready")
        y_made, y_ready = sem("y_made"), sem("y_ready")
        added = sem("added")

        def batches(eng, body):
            body(0, 0, 0)
            with eng.Fori(0, (B - 2) // 2) as it:
                body(it * 2 + 1, 1, it)
                body(it * 2 + 2, 0, it + 1)
            body(B - 1, 1, (B - 1) // 2)

        def blocks(eng, body):
            for b in range(AHEAD + 1):
                body(b, b, 0)
            with eng.Fori(0, (NB - AHEAD - 1) // RING) as it:
                for b in range(AHEAD + 1, AHEAD + 1 + RING):
                    body(it * RING + b, b % RING, it + b // RING)

        block = st.enter_context(nc.Block())

        @block.sync
        def _(sp):
            def load_x(i, u):
                sp.dma_start(x_sb[u][:, :, :], x[bass.ds(i * S, S), :].rearrange("(t p) d -> p t d", p=TT)).then_inc(x_loaded[u], 16)

            def load_ctx(i, u, c):
                sp.dma_start(ctx_sb[u][:, c, :], ctx[bass.ds(i * C + c * CR, CR), :]).then_inc(ctx_loaded[u][c], 16)

            load_x(0, 0)
            for c in range(NC):
                load_ctx(0, 0, c)
            for n, g in enumerate((g_xattn, g_ffn)):
                sp.dma_start(g_raw[:, n:n + 1], g.rearrange("(a n) -> a n", a=1).to_broadcast([P, 1])).then_inc(small_loaded, 16)
            sp.dma_start(gate[:, :, :], gate_w.rearrange("(k p) e -> p k e", p=P)).then_inc(small_loaded, 16)
            load_x(1, 1)
            for c in range(NC):
                load_ctx(1, 1, c)
            sp.wait_ge(consts, 1)
            sp.dma_start(table.rearrange("(p n) c -> p n c", p=P), init_t[:, :, :]).then_inc(table_ready, 16)
            sp.dma_start(out[T:T + P, :], zeros[:, :]).then_inc(table_ready, 16)
            sp.dma_start(xf_dram[T:T + P, :], zeros[:, :]).then_inc(table_ready, 16)

            def load_weights(e):
                for src, at in ((w1, 0), (w3, HID)):
                    dst = w13[:, bass.ds(e * KD * 2 * HID, KD * 2 * HID)].rearrange("p (k n) -> p k n", k=KD)[:, :, at:at + HID]
                    sp.dma_start(dst, src[bass.ds(e * D, D), :].rearrange("(k p) n -> p k n", p=P)).then_inc(w_loaded, 16)
                dst = w2s[:, bass.ds(e * KH * D, KH * D)].rearrange("p (k n) -> p k n", k=KH)
                sp.dma_start(dst, w2[bass.ds(e * HID, HID), :].rearrange("(k p) n -> p k n", p=P)).then_inc(w_loaded, 16)

            def store_rows(j, v, hj):
                sp.wait_ge(x2_ready, j * 2 + 2)
                sp.dma_start(out[bass.ds(j * S, S), :].rearrange("(t p) d -> p t d", p=TT), x2[v][:, :, :]).then_inc(x2_stored[v], 16)
                sp.wait_ge(xf_ready, j * 2 + 2)
                sp.dma_start(xf_dram[bass.ds(j * S, S), :].rearrange("(t p) d -> p t d", p=TT), xf[v][:, :, :]).then_inc(xf_stored[v], 16)

            def step(i, u, h):
                first_, last = isinstance(i, int) and i == 0, isinstance(i, int) and i == B - 1
                if u == 0:
                    load_weights(h)
                if not first_:
                    sp.wait_ge(x2_ready, i * 2)
                    if not last:
                        load_x(i + 1, 1 - u)
                    store_rows(i - 1, 1 - u, None)
                if not last:
                    for c in range(NC):
                        sp.wait_ge(attn_part, i * NC + c + 1)
                        load_ctx(i + 2, u, c)

            step(0, 0, 0)
            with sp.Fori(0, (B - 4) // 2) as it:
                step(it * 2 + 1, 1, it)
                step(it * 2 + 2, 0, it + 1)
            step_tail = B - 3
            step(step_tail, 1, None)
            for i in (B - 2, B - 1):
                u = i % 2
                if u == 0:
                    load_weights(i // 2)
                sp.wait_ge(x2_ready, i * 2)
                if i < B - 1:
                    load_x(i + 1, 1 - u)
                store_rows(i - 1, 1 - u, None)
            store_rows(B - 1, 1, None)
            for v in range(2):
                sp.wait_ge(x2_stored[v], 16 * B // 2)
                sp.wait_ge(xf_stored[v], 16 * B // 2)
            sp.nop().then_inc(phase2, 1)

            sp.wait_ge(map_ready, 1)
            for v in range(2):
                sp.wait_ge(routed[v], 16 * 2 * TOPK * B // 2)

            def load_meta(b, n):
                if not (isinstance(b, int) and b < RING):
                    sp.wait_ge(added, b * 16 - (RING - 1) * 16)
                row = sp.value_load(bmap[0:1, 1, bass.ds(b, 1)], min_val=0, max_val=TRASH)
                sp.dma_start(meta[n][:, :], table[bass.ds(row * P, P), :]).then_inc(meta_loaded[n], 16)

            for b in range(RING):
                load_meta(b, b)
            with sp.Fori(1, NBM // RING) as it:
                for n in range(RING):
                    load_meta(it * RING + n, n)
            for b in range(NBM - NBM % RING, NBM):
                load_meta(b, b % RING)
            sp.wait_ge(added, 16 * NB)

        @block.gpsimd
        def _(pool):
            seq = Seq(pool, pool_seq)
            g = nc.gpsimd
            seq.done(g.memset(ident[:, :], 0.0))
            seq.done(g.memset(lower[:, :], 1.0))
            seq.done(g.memset(ones[:, :], 1.0))
            seq.done(g.memset(zeros[:, :], 0.0))
            seq.done(g.memset(neg_half[:, :], -0.5))
            seq.done(g.memset(euler[:, :], float(np.e)))
            seq.done(g.memset(R[:, :, :], 0.0))
            seq.done(g.iota(iota_e[:, :], pattern=[[1, E]], base=0, channel_multiplier=0, allow_small_or_imprecise_dtypes=True))
            seq.done(g.iota(ebase[:, :], pattern=[[T, E]], base=0, channel_multiplier=0, allow_small_or_imprecise_dtypes=True))
            seq.done(g.iota(tok[:, :], pattern=[[TT, 2]], base=0, channel_multiplier=1, allow_small_or_imprecise_dtypes=True))
            seq.done(g.iota(bidx[:, :], pattern=[[1, NBM]], base=0, channel_multiplier=0, allow_small_or_imprecise_dtypes=True))
            seq.done(g.iota(init_i[:, :], pattern=[[1, TRASH + 1]], base=0, channel_multiplier=TRASH + 1))
            seq.done(g.memset(init_t[:, :, :], 0))
            seq.settle()
            seq.done(g.affine_select(out=ident[:, :], in_=ident[:, :], compare_op=ALU.not_equal, fill=1.0, base=0, pattern=[[-1, P]], channel_multiplier=1))
            seq.done(g.affine_select(out=lower[:, :], in_=lower[:, :], compare_op=ALU.is_gt, fill=0.0, base=0, pattern=[[1, TT]], channel_multiplier=-1))
            seq.settle()

            def inv_std(mv, at, ready, out_ready, n):
                hold(pool, ready, n)
                seq.done(g.tensor_scalar(ve[:, at:at + 2], mv[:, :, 1], EPS, None, ALU.add))
                seq.settle()
                g.tensor_tensor(rstd[:, at:at + 2], ve[:, at:at + 2], neg_half[:, at:at + 2], ALU.pow).then_inc(out_ready, 1)

            def route_batch(j, v, n):
                pool.wait_ge(dl_ready, n)
                g.tensor_tensor(ex[:, :, :].rearrange("p t e -> p (t e)"), euler[:, :], dl[:, :, :].rearrange("p t e -> p (t e)"), ALU.pow).then_inc(ex_ready, 1)
                hold(pool, route_ready, n)
                for t in range(2):
                    for k in range(TOPK):
                        m = t * TOPK + k
                        g.indirect_dma_start(out=table, out_offset=bass.IndirectOffsetOnAxis(ap=pos_i[v][:, m:m + 1], axis=0),
                                             in_=route[v][:, t, k, :], in_offset=None).then_inc(routed[v], 16)

            inv_std(mv1, 0, mv1_ready, rstd1_ready, 1)
            pool.wait_ge(table_ready, 48)

            def step(i, u, base):
                seq.base, seq.n = base, 0
                first_, last = isinstance(i, int) and i == 0, isinstance(i, int) and i == B - 1
                if not first_:
                    inv_std(mv2, 2, mv2_ready, rstd2_ready, i)
                if not last:
                    inv_std(mv1, 0, mv1_ready, rstd1_ready, i + 2)
                if not first_:
                    route_batch(i - 1, 1 - u, i)
                return seq.n

            at = seq.base + seq.n
            at += step(0, 0, at)
            PER = 2
            with pool.Fori(0, (B - 2) // 2) as it:
                assert step(it * 2 + 1, 1, it * (2 * PER) + at) == PER
                step(it * 2 + 2, 0, it * (2 * PER) + (at + PER))
            at += PER * (B - 2)
            at += step(B - 1, 1, at)
            seq.base, seq.n = at, 0
            inv_std(mv2, 2, mv2_ready, rstd2_ready, B)
            route_batch(B - 1, 1, B)

            pool.wait_ge(phase2, 1)
            for v in range(2):
                pool.wait_ge(routed[v], 16 * 2 * TOPK * B // 2)

            def gather(b, n, lap):
                hold(pool, meta_loaded[n], lap * 16 + 16)
                g.indirect_dma_start(out=xg[n % 2][:, :], out_offset=None, in_=xf_dram,
                                     in_offset=bass.IndirectOffsetOnAxis(ap=meta[n][:, 0:1], axis=0)).then_inc(gathered[n % 2], 16)

            def scatter(b, n):
                pool.wait_ge(y_ready, b + 1)
                if not (isinstance(b, int) and b == 0):
                    hold(pool, added, b * 16)
                g.indirect_dma_start(out=out, out_offset=bass.IndirectOffsetOnAxis(ap=meta[n][:, 0:1], axis=0),
                                     in_=y_sb[n % 2][:, :], in_offset=None, compute_op=ALU.add).then_inc(added, 16)

            for b in range(AHEAD):
                gather(b, b, 0)

            def step2(b, n, lap):
                pool.wait_ge(xgT_made, b + 1)
                gather(b + AHEAD, (n + AHEAD) % RING, lap + (n + AHEAD) // RING)
                if not (isinstance(b, int) and b == 0):
                    scatter(b - 1, (n - 1) % RING)

            blocks(pool, step2)
            scatter(NB - 1, (NB - 1) % RING)
            for u in range(2):
                pool.wait_ge(gathered[u], 16 * ((NBM + 1 - u) // 2))
            pool.wait_ge(added, 16 * NB)

        @block.scalar
        def _(act):
            a = nc.scalar
            act.wait_ge(small_loaded, 48)
            a.activation(g_tanh[:, :], g_raw[:, :], ACT.Tanh).then_inc(tanh_ready, 1)

            def ctxT_out(i, u, c):
                n = i * NC + c
                act.wait_ge(ctxT_made, n + 1)
                a.activation(ctxT[u][:, :, c * CR:(c + 1) * CR], T_ps[c % 2][:, 0:KD * CR].rearrange("p (k r) -> p k r", k=KD), ACT.Copy).then_inc(ctxT_ready, 1)

            def gelu(i, c):
                n = i * NC + c
                act.wait_ge(h_made, n + 1)
                if not (isinstance(i, int) and i == 0):
                    act.wait_ge(attn_part, n + 1 - NC)
                a.activation(aT[:, c, :], H_ps[c % 2][0:CR, 0:S], ACT.Gelu_apprx_tanh).then_inc(a_ready, 1)

            for c in range(NC):
                ctxT_out(0, 0, c)

            def step(i, u, h):
                last = isinstance(i, int) and i == B - 1
                for c in range(NC):
                    if not last:
                        ctxT_out(i + 1, 1 - u, c)
                    gelu(i, c)

            batches(act, step)

            def y_out(b, u):
                act.wait_ge(y_made, b + 1)
                if not (isinstance(b, int) and b < 2):
                    act.wait_ge(added, (b - 1) * 16)
                a.activation(y_sb[u][:, :], O_ps[u][:, :], ACT.Copy, scale=g_tanh[:, 1:2]).then_inc(y_ready, 1)

            def step2(b, n, lap):
                first_, u = isinstance(b, int) and b == 0, n % 2
                if not first_:
                    act.wait_ge(hhT_made, b)
                    a.activation(hhT, bank[6][:, 0:KH * P], ACT.Copy).then_inc(hhT_ready, 1)
                act.wait_ge(up_made, b + 1)
                if not first_:
                    act.wait_ge(hh_ready, b)
                a.activation(sg, H_ps[u][:, 0:HID], ACT.Silu, scale=score[n]).then_inc(sg_ready, 1)
                if not first_:
                    y_out(b - 1, 1 - u)

            blocks(act, step2)
            act.wait_ge(hhT_made, NB)
            a.activation(hhT, bank[6][:, 0:KH * P], ACT.Copy).then_inc(hhT_ready, 1)
            y_out(NB - 1, (NB - 1) % 2)

        @block.vector
        def _(dve):
            v = nc.vector
            seq = Seq(dve, dve_seq)
            dve.wait_ge(pool_seq, 15)
            seq.done(v.tensor_scalar(init_i[:, :], init_i[:, :], P - 1, None, ALU.bitwise_and))
            seq.settle()
            v.tensor_scalar(init_t[:, :, 0], init_i[:, :], float(T), None, ALU.add).then_inc(consts, 1)

            def norm_stats(src, mv, ready):
                for t in range(2):
                    seq.done(v.bn_stats(stats[:, t, :], src[:, t, :]))
                seq.settle()
                for t in range(2):
                    last = v.bn_aggr(mv[:, t, :], stats[:, t, :])
                    if t == 0:
                        seq.done(last)
                last.then_inc(ready, 1)

            def ln1(i, u, n_x, first_):
                dve.wait_ge(x_loaded[u], n_x)
                norm_stats(x_sb[u], mv1, mv1_ready)
                dve.wait_ge(mv1_ready, i + 1)
                dve.wait_ge(rstd1_ready, i + 1)
                if not first_:
                    dve.wait_ge(small_made, 2 if isinstance(i, int) and i == 1 else i * 4 - 4)
                for t in range(2):
                    v.tensor_scalar(xn[:, t, :], x_sb[u][:, t, :], mv1[:, t, 0:1], rstd[:, t:t + 1], ALU.subtract, ALU.mult).then_inc(xn_ready, 1)

            def residual_ln2(j, v_, hj, first2):
                dve.wait_ge(attn_part, j * NC + NC)
                dve.wait_ge(x2_stored[v_], hj * 16)
                for t in range(2):
                    v.scalar_tensor_tensor(x2[v_][:, t, :], O_ps[t][0:TT, :], g_tanh[0:TT, 0:1], x_sb[v_][:, t, :], ALU.mult, ALU.add).then_inc(x2_ready, 1)
                dve.wait_ge(x2_ready, j * 2 + 2)
                norm_stats(x2[v_], mv2, mv2_ready)
                dve.wait_ge(mv2_ready, j + 1)
                dve.wait_ge(rstd2_ready, j + 1)
                dve.wait_ge(xf_stored[v_], hj * 16)
                for t in range(2):
                    v.tensor_scalar(xf[v_][:, t, :], x2[v_][:, t, :], mv2[:, t, 0:1], rstd[:, 2 + t:3 + t], ALU.subtract, ALU.mult).then_inc(xf_ready, 1)

            def small_out(idx, dst):
                dve.wait_ge(small_made, idx + 1)
                v.tensor_copy(dst, X_ps[:, 0:KD * TT].rearrange("p (k r) -> p k r", k=KD)).then_inc(small_ready, 1)

            def route_top(j):
                dve.wait_ge(logits_made, j + 1)
                seq.done(v.tensor_copy(lg[:, :, :].rearrange("p t e -> p (t e)"), lg_ps))
                seq.settle()
                for t in range(2):
                    seq.done(v.max(mx[:, t, :], lg[:, t, :]))
                seq.settle()
                for t in range(2):
                    seq.done(v.max_index(ix[:, t, :], mx[:, t, :], lg[:, t, :]))
                    v_last = v.tensor_scalar(dl[:, t, :], mx[:, t, :], mx[:, t, 0:1], None, ALU.subtract)
                    if t == 0:
                        seq.done(v_last)
                v_last.then_inc(dl_ready, 1)
                seq.settle()
                seq.done(v.tensor_copy(ixf[:, :, :], ix[:, :, 0:TOPK]))
                seq.settle()
                for t in range(2):
                    for k in range(TOPK):
                        seq.done(v.tensor_scalar(oh[:, t, k, :], iota_e[:, :], ixf[:, t, k:k + 1], None, ALU.is_equal))
                seq.settle()
                seq.done(v.tensor_tensor(M[:, :, :], oh[:, :, 0, :], oh[:, :, 1, :], ALU.add))
                seq.settle()
                v.tensor_tensor(R[:, 1, :], R[:, 0, :], M[:, 0, :], ALU.add).then_inc(mask_ready, 1)

            def route_scores(j, v_, hj):
                dve.wait_ge(ex_ready, j + 1)
                seq.done(v.reduce_sum(sm[:, :], ex[:, :, :], AX.X))
                seq.settle()
                seq.done(v.reciprocal(rs[:, :], sm[:, :]))
                dve.wait_ge(routed[v_], hj * (16 * 2 * TOPK))
                for k in range(TOPK):
                    seq.done(v.tensor_copy(route[v_][:, :, k, 0], tok[:, :]))
                seq.settle()
                for t in range(2):
                    seq.done(v.tensor_scalar(route[v_][:, t, :, 1].bitcast(F32), ex[:, t, 0:TOPK], rs[:, t:t + 1], None, ALU.mult))
                seq.done(v.tensor_scalar(tok[:, :], tok[:, :], float(S), None, ALU.add))

            def route_pos(j, v_):
                dve.wait_ge(rank_made, j + 1)
                v.tensor_tensor(R[:, 0, :], R[:, 1, :], M[:, 1, :], ALU.add).then_inc(dve_seq, 1)
                seq.n += 1
                for t in range(2):
                    ins = v.tensor_tensor(pos_e[:, t, :], rk_ps[:, t * E:(t + 1) * E], ebase[:, :], ALU.add)
                    if t == 0:
                        seq.done(ins)
                ins.then_inc(pos_read, 1)
                dve.wait_ge(pos_read, j + 1)
                seq.settle()
                for k in range(TOPK):
                    seq.done(v.tensor_tensor(pos_o[:, :, k, :], pos_e[:, :, :], oh[:, :, k, :], ALU.mult))
                seq.settle()
                seq.done(v.reduce_sum(pos_f[:, :], pos_o[:, :, :, :].rearrange("p t k e -> p (t k) e"), AX.X))
                seq.settle()
                v.tensor_copy(pos_i[v_][:, :], pos_f[:, :]).then_inc(route_ready, 1)

            ln1(0, 0, 16, True)
            dve.wait_ge(tanh_ready, 1)
            for t in range(2):
                small_out(t, xnT[0][:, :, t * TT:(t + 1) * TT])

            def step(i, u, h, base):
                seq.base, seq.n = base, 0
                first_, last = isinstance(i, int) and i == 0, isinstance(i, int) and i == B - 1
                hj = h if u else h - 1
                if not first_:
                    residual_ln2(i - 1, 1 - u, hj, None)
                if not last:
                    ln1(i + 1, 1 - u, (h + 1) * 16 + 16 if u else h * 16 + 16, False)
                if not first_:
                    for t in range(2):
                        small_out(i * 4 + t, xfT[:, t, :, :])
                if not last:
                    for t in range(2):
                        small_out(i * 4 + 2 + t, xnT[1 - u][:, :, t * TT:(t + 1) * TT])
                if not first_:
                    route_top(i - 1)
                    route_scores(i - 1, 1 - u, hj)
                    route_pos(i - 1, 1 - u)
                return seq.n

            at = seq.base + seq.n
            at += step(0, 0, 0, at)
            PER = DVE_STEPS
            with dve.Fori(0, (B - 2) // 2) as it:
                got = step(it * 2 + 1, 1, it, it * (2 * PER) + at)
                assert got == PER, got
                step(it * 2 + 2, 0, it + 1, it * (2 * PER) + (at + PER))
            at += PER * (B - 2)
            at += step(B - 1, 1, (B - 1) // 2, at)
            seq.base, seq.n = at, 0
            residual_ln2(B - 1, 1, (B - 1) // 2, None)
            for t in range(2):
                small_out((B - 1) * 4 + 2 + t, xfT[:, t, :, :])
            route_top(B - 1)
            route_scores(B - 1, 1, (B - 1) // 2)
            route_pos(B - 1, 1)

            def one(ins):
                seq.done(ins)
                seq.settle()

            dve.wait_ge(counts_made, 1)
            one(v.tensor_scalar(cnt_i[:, :], cnt_ps[0:1, :], float(P - 1), None, ALU.add))
            one(v.tensor_scalar(cnt_i[:, :], cnt_i[:, :], P.bit_length() - 1, None, ALU.logical_shift_right))
            one(v.tensor_copy(nblk[:, :], cnt_i[:, :]))
            one(v.memset(first[:, :], 0.0))
            for e in range(E):
                one(v.tensor_tensor(first[:, e + 1:e + 2], first[:, e:e + 1], nblk[:, e:e + 1], ALU.add))
            one(v.tensor_scalar(gap[:, :], nblk[:, :], -1.0, float(EB), ALU.mult, ALU.add))
            one(v.memset(m_e[:, :], 0.0))
            one(v.tensor_copy(m_r[:, :], bidx[:, :]))
            for e in range(1, E):
                seq.done(v.scalar_tensor_tensor(m_e[:, :], bidx[:, :], first[:, e:e + 1], m_e[:, :], ALU.is_ge, ALU.add))
                one(v.tensor_scalar(m_t[:, :], bidx[:, :], first[:, e:e + 1], gap[:, e - 1:e], ALU.is_ge, ALU.mult))
                one(v.tensor_tensor(m_r[:, :], m_r[:, :], m_t[:, :], ALU.add))
            seq.done(v.tensor_scalar(m_r[:, :], m_r[:, :], float(-TRASH), None, ALU.add))
            one(v.tensor_scalar(m_t[:, :], bidx[:, :], first[:, E:E + 1], None, ALU.is_lt))
            one(v.tensor_tensor(m_r[:, :], m_r[:, :], m_t[:, :], ALU.mult))
            seq.done(v.tensor_copy(bmap[:, 0, :], m_e[:, :]))
            one(v.tensor_scalar(bmap[:, 1, :], m_r[:, :], float(TRASH), None, ALU.add))
            v.engine_nop().then_inc(map_ready, 1)

            def xgT_out(b, u):
                dve.wait_ge(xgT_made, b + 1)
                v.tensor_copy(xgT[u], T_ps[u][:, :]).then_inc(xgT_ready, 1)

            xgT_out(0, 0)

            def step2(b, n, lap):
                u = n % 2
                xgT_out(b + 1, 1 - u)
                dve.wait_ge(sg_ready, b + 1)
                if not (isinstance(b, int) and b == 0):
                    dve.wait_ge(hhT_made, b)
                v.scalar_tensor_tensor(hh, H_ps[u][:, HID:2 * HID], score[n], sg, ALU.mult, ALU.mult).then_inc(hh_ready, 1)

            blocks(dve, step2)

        @block.tensor
        def _(pe):
            t_ = nc.tensor
            pe.wait_ge(pool_seq, 15)

            def trans_ctx(i, u, c, n_ctx, first_):
                n = i * NC + c
                pe.wait_ge(ctx_loaded[u][c], n_ctx)
                if not (first_ and c < 2):
                    pe.wait_ge(ctxT_ready, n - 1)
                for k in range(KD):
                    ins = t_.transpose(T_ps[c % 2][:, k * CR:(k + 1) * CR], ctx_sb[u][:, c, k * P:(k + 1) * P], ident[0:CR, 0:CR])
                ins.then_inc(ctxT_made, 1)

            def small_trans(idx, src, first_):
                if not first_:
                    pe.wait_ge(small_ready, idx)
                for k in range(KD):
                    ins = t_.transpose(X_ps[:, k * TT:(k + 1) * TT], src[:, k * P:(k + 1) * P], ident[0:TT, 0:TT])
                ins.then_inc(small_made, 1)

            def mm1(i, u, c, first_):
                n = i * NC + c
                if c == 0:
                    pe.wait_ge(small_ready, i * 4 if not first_ else 2)
                pe.wait_ge(ctxT_ready, n + 1)
                if not (first_ and c < 2):
                    pe.wait_ge(a_ready, n - 1)
                for k in range(KD):
                    ins = t_.matmul(H_ps[c % 2][0:CR, 0:S], ctxT[u][:, k, c * CR:(c + 1) * CR], xnT[u][:, k, :], start=k == 0, stop=k == KD - 1)
                ins.then_inc(h_made, 1)

            def mm2(i, u, c, first_):
                n = i * NC + c
                pe.wait_ge(a_ready, n + 1)
                if c == 0 and not first_:
                    pe.wait_ge(x2_ready, i * 2)
                for t in range(2):
                    ins = t_.matmul(O_ps[t][0:TT, :], aT[:, c, t * TT:(t + 1) * TT], ctx_sb[u][:, c, :], start=c == 0, stop=c == NC - 1)
                ins.then_inc(attn_part, 1)

            def logits(j):
                pe.wait_ge(small_ready, 4 * B if isinstance(j, int) and j == B - 1 else j * 4 + 6)
                if not (isinstance(j, int) and j == 0):
                    pe.wait_ge(pos_read, j)
                for t in range(2):
                    for k in range(KD):
                        ins = t_.matmul(lg_ps[:, t * E:(t + 1) * E], xfT[:, t, k, :], gate[:, k, :], start=k == 0, stop=k == KD - 1)
                ins.then_inc(logits_made, 1)

            def rank(j):
                pe.wait_ge(mask_ready, j + 1)
                t_.matmul(rk_ps, lower[:, :], M[:, :, :].rearrange("p t e -> p (t e)"), start=True, stop=False)
                t_.matmul(rk_ps, ones[:, 0:TT], R[:, :, :].rearrange("p t e -> p (t e)"), start=False, stop=True).then_inc(rank_made, 1)

            pe.wait_ge(small_loaded, 48)
            for c in range(NC):
                trans_ctx(0, 0, c, 16, True)
            for t in range(2):
                pe.wait_ge(xn_ready, t + 1)
                small_trans(t, xn[:, t, :], t == 0)

            def step(i, u, h):
                first_, last = isinstance(i, int) and i == 0, isinstance(i, int) and i == B - 1
                for c in range(NC):
                    if not last:
                        trans_ctx(i + 1, 1 - u, c, h * 16 + 16 if not u else h * 16 + 32, False)
                    mm1(i, u, c, first_)
                    if c >= 2:
                        mm2(i, u, c - 2, first_)
                    if c in (1, 2) and not first_:
                        pe.wait_ge(xf_ready, i * 2 - 2 + c)
                        small_trans(i * 4 + c - 1, xf[1 - u][:, c - 1, :], False)
                    if c in (3, 4) and not last:
                        pe.wait_ge(xn_ready, i * 2 + c)
                        small_trans(i * 4 + c - 1, xn[:, c - 3, :], False)
                    if c == 4 and not first_:
                        logits(i - 1)
                mm2(i, u, NC - 2, first_)
                if not first_:
                    rank(i - 1)
                mm2(i, u, NC - 1, first_)

            batches(pe, step)
            for t in range(2):
                pe.wait_ge(xf_ready, 2 * B - 1 + t)
                small_trans((B - 1) * 4 + 2 + t, xf[1][:, t, :], False)
            logits(B - 1)
            rank(B - 1)
            pe.wait_ge(route_ready, B)
            t_.matmul(cnt_ps, ones[:, :], R[:, 0, :], start=True, stop=True).then_inc(counts_made, 1)

            pe.wait_ge(w_loaded, 16 * 3 * E)
            pe.wait_ge(map_ready, 1)

            def trans_rows(b, u, n_g, first_):
                pe.wait_ge(gathered[u], n_g)
                if not first_:
                    pe.wait_ge(xgT_ready, b - 1)
                for k in range(KD):
                    ins = t_.transpose(T_ps[u][:, k * P:(k + 1) * P], xg[u][:, k * P:(k + 1) * P], ident[:, :])
                ins.then_inc(xgT_made, 1)

            def trans_hid(b):
                pe.wait_ge(hh_ready, b + 1)
                if not (isinstance(b, int) and b == 0):
                    pe.wait_ge(hhT_ready, b)
                for k in range(KH):
                    ins = t_.transpose(bank[6][:, k * P:(k + 1) * P], hh[:, k * P:(k + 1) * P], ident[:, :])
                ins.then_inc(hhT_made, 1)

            def up(b, u, e, first2):
                pe.wait_ge(xgT_ready, b + 1)
                if not first2:
                    pe.wait_ge(hh_ready, b - 1)
                for k in range(KD):
                    ins = t_.matmul(H_ps[u][:, :], xgT[u][:, k * P:(k + 1) * P], w13[:, bass.ds(e * (KD * 2 * HID) + k * 2 * HID, 2 * HID)], start=k == 0, stop=k == KD - 1)
                ins.then_inc(up_made, 1)

            def down(b, u, e, first2):
                pe.wait_ge(hhT_ready, b + 1)
                if not first2:
                    pe.wait_ge(y_ready, b - 1)
                for k in range(KH):
                    ins = t_.matmul(O_ps[u][:, :], hhT[:, k * P:(k + 1) * P], w2s[:, bass.ds(e * (KH * D) + k * D, D)], start=k == 0, stop=k == KH - 1)
                ins.then_inc(y_made, 1)

            def expert(b):
                return pe.value_load(bmap[0:1, 0, bass.ds(b, 1)], min_val=0, max_val=E - 1)

            trans_rows(0, 0, 16, True)

            def step2(b, n, lap):
                u = n % 2
                h = lap * (RING // 2) + n // 2
                if isinstance(b, int) and b == 0:
                    trans_rows(1, 1, 16, True)
                    up(0, 0, expert(0), True)
                    return
                trans_hid(b - 1)
                trans_rows(b + 1, 1 - u, h * 16 + 32 if u else h * 16 + 16, False)
                small = isinstance(b, int)
                up(b, u, expert(b), small and b < 2)
                down(b - 1, 1 - u, expert(b - 1), small and b - 1 < 2)

            blocks(pe, step2)
            trans_hid(NB - 1)
            down(NB - 1, (NB - 1) % 2, expert(NB - 1), False)


DVE_STEPS = 30


_INS = ['x', 'ctx_1024', 'g_xattn', 'g_ffn', 'L0_ffn_gate_w', 'L0_ffn_w1', 'L0_ffn_w2', 'L0_ffn_w3']


def kernel(**inputs):
    import concourse.bacc as _bacc
    from concourse.bass_utils import run_bass_kernel_spmd as _run

    nc = _bacc.Bacc("TRN2", target_bir_lowering=False, num_devices=1)
    arrays, args = {}, []
    for name in _INS:
        a = np.ascontiguousarray(inputs[name])
        if a.ndim == 3:
            a = a.reshape(-1, a.shape[-1])
        arrays[f"in_{name}"] = a
        args.append(nc.dram_tensor(f"in_{name}", a.shape, mybir.dt.from_np(a.dtype), kind="ExternalInput").ap())
    args.append(nc.dram_tensor("out_rows", (T + P, D), F32, kind="ExternalOutput").ap())
    build(nc, *args)
    r = _run(nc, [arrays], core_ids=[0])
    return r.results[0]["out_rows"][:T].reshape(B, S, D)
```

```python
import concourse.bass as bass
from concourse import mybir
from contextlib import ExitStack
import numpy as np

F32 = mybir.dt.float32
F16 = mybir.dt.float16
I32 = mybir.dt.int32
U32 = mybir.dt.uint32
ALU = mybir.AluOpType
ACT = mybir.ActivationFunctionType
AX = mybir.AxisListType

B, S, D = 16, 224, 512
C = 750
E, HID, TOPK = 8, 256, 2
T = B * S
EPS = 1e-5

X_BITS = 10
TOP = 15
BIAS, MANT = 127, 23
HID_BITS = TOP - 2 * ((D - 1).bit_length() + TOP)
PARTS = ((0, 0), (0, 1), (1, 0))
A_BITS = -(D.bit_length() // 2)
ROOT = (BIAS + 1) // 2

P = 128
TT = S // 2
CR, NC = 125, 6
NQ = NC // 2
CS = CR + 1
KD = D // P
KH = HID // P
EB = T // P
TRASH = E * EB
NB = (T * TOPK) // P + E - 1
PEEL = 3
AHEAD = 3
PEEL2 = 3
NBM = NB + AHEAD
RING = 6
assert (NB - PEEL2) % RING == 0 and RING % AHEAD == 0 and RING % 2 == 0


def hold(eng, sem, value):
    eng.wait_ge(sem, value)
    eng.nop(nofuse=True)


def later(i, n):
    return not isinstance(i, int) or i >= n


class Seq:

    def __init__(self, eng, sem, base=0):
        self.eng, self.sem, self.base, self.n = eng, sem, base, 0

    def done(self, ins):
        self.n += 1
        return ins.then_inc(self.sem, 1)

    def hold(self):
        hold(self.eng, self.sem, self.base + self.n)

    def settle(self):
        self.eng.wait_ge(self.sem, self.base + self.n)


def build(nc, x, ctx, g_xattn, g_ffn, gate_w, w1, w2, w3, out):
    xf_dram = nc.dram_tensor("xf_rows", (T + P, D), F32).ap()
    table = nc.dram_tensor("route_table", ((TRASH + 1) * P, 2), I32).ap()

    st = ExitStack()
    with st:
        def sb(name, shape, dt=F32):
            return st.enter_context(nc.sbuf_tensor(name, shape, dt))

        def ps(name, shape, dt=F32):
            return st.enter_context(nc.psum_tensor(name, shape, dt))

        def sem(name):
            return st.enter_context(nc.semaphore(name))

        w13 = sb("w13", [P, E * KD * 2 * 2 * HID], F16)
        w2s = sb("w2s", [P, E * KH * 2 * D], F16)
        w_raw = sb("w_raw", [P, KD * HID])
        w_sum = sb("w_sum", [P, 1])
        w_gsum = sb("w_gsum", [P, 1])
        w_s = sb("w_s", [P, 1], I32)
        w_si = sb("w_si", [P, 1], I32)
        w_inv = sb("w_inv", [P, 3, E], I32)
        w1_s = sb("w1_s", [P, E])
        q_tmp = w_raw[:, 0:2 * E].rearrange("p (n e) -> p n e", n=2)
        Q = sb("Q", [P, E * 3])
        cols = [sb(f"cols{u}", [P, 3]) for u in range(2)]
        gate = sb("gate", [P, KD, E])
        ident = sb("ident", [P, P])
        ident16 = sb("ident16", [P, P], F16)
        lower = sb("lower", [TT, TT])
        ones = sb("ones", [TT, P])
        iota_e = sb("iota_e", [TT, E])
        ebase = sb("ebase", [TT, E])
        tok = sb("tok", [TT, 2])
        neg_half = sb("neg_half", [TT, 4])
        euler = sb("euler", [TT, 2 * E])
        g_raw = sb("g_raw", [P, 2])
        g_tanh = sb("g_tanh", [P, 2])
        ctx_raw = sb("ctx_raw", [P, NC, D])
        ctx_part = [[sb(f"ctx_part{u}{h}", [CR, NC, D], F16) for h in range(2)] for u in range(2)]
        ctxT_buf = [sb(f"ctxT{u}", [P, 2 * KD * NC * CS], F16) for u in range(2)]
        ctxT = [b[:, :].rearrange("p (g c) -> p g c", g=2 * KD) for b in ctxT_buf]
        squares = [sb(f"squares{n}", [P, KD * HID], F16) for n in range(2)]
        ctx_sum = sb("ctx_sum", [P, NQ])
        ctx_gsum = sb("ctx_gsum", [P, NQ])
        ctx_max = sb("ctx_max", [P, 1])
        exp_f = sb("exp_f", [P, 2])
        exp_i = exp_f[:, 1:2].bitcast(I32)
        ctx_s = [sb(f"ctx_s{u}", [P, 1], I32) for u in range(2)]
        ctx_inv = [sb(f"ctx_inv{u}", [P, 1], I32) for u in range(2)]
        tanh_a = sb("tanh_a", [P, 1])
        factors = sb("factors", [P, 6])
        a_s = [factors[:, u:u + 1] for u in range(2)]
        h_s = [factors[:, 2 + u:3 + u] for u in range(2)]
        o_s = [factors[:, 4 + u:5 + u] for u in range(2)]
        x_sb = [sb(f"x{u}", [TT, 2, D]) for u in range(2)]
        xn = sb("xn", [TT, 2, D])
        xnT = [sb(f"xnT{u}", [P, 2, KD, S], F16) for u in range(2)]
        a_f = [sb(f"a_f{u}", [CR, 2 * S]) for u in range(2)]
        a_part = [sb(f"a_part{h}", [CR, NC, S], F16) for h in range(2)]
        x2 = sb("x2", [TT, 2, D])
        xf = sb("xf", [TT, 2, D])
        xfT = sb("xfT", [P, 2, KD, TT])
        stats = sb("stats", [TT, 2, 6])
        mv1 = sb("mv1", [TT, 2, 2])
        mv2 = sb("mv2", [TT, 2, 2])
        ve = sb("ve", [TT, 4])
        rstd = sb("rstd", [TT, 4])
        lg = sb("lg", [TT, 2, E])
        mx = sb("mx", [TT, 2, 8])
        ix = sb("ix", [TT, 2, 8], U32)
        ixf = sb("ixf", [TT, 2, TOPK])
        oh = sb("oh", [TT, 2, TOPK, E])
        M = sb("M", [TT, 2, E])
        R = sb("R", [TT, 2, E])
        dl = sb("dl", [TT, 2, E])
        ex = sb("ex", [TT, 2, E])
        sm = sb("sm", [TT, 2])
        rs = sb("rs", [TT, 2])
        pos_e = sb("pos_e", [TT, 2, E])
        pos_o = sb("pos_o", [TT, 2, TOPK, E])
        pos_f = sb("pos_f", [TT, 2 * TOPK])
        pos_i = [sb(f"pos_i{u}", [TT, 2 * TOPK], I32) for u in range(2)]
        route = [sb(f"route{u}", [TT, 2, TOPK, 2], I32) for u in range(2)]
        gap = xn[0:1, 1, 0:E]
        cnt_i = xn[0:1, 1, E:2 * E].bitcast(I32)
        sums = xn[0:1, 1, 2 * E:2 * E + 4 * (E // 2 + E + 1)].rearrange("p (n c) -> p n c", n=4)
        is_from, skipped = (x_sb[0][0:1, n, 0:(E - 1) * NBM].rearrange("p (e b) -> p e b", e=E - 1) for n in range(2))
        bidx = sb("bidx", [1, NBM])
        m_e, m_r, m_t = (xn[0:1, 0, n * NBM:(n + 1) * NBM] for n in range(3))
        bmap = sb("bmap", [1, 2, NBM], I32)
        meta_all = sb("meta", [P, RING, 2], I32)
        meta = [meta_all[:, n, :] for n in range(RING)]
        score = [meta[n][:, 1:2].bitcast(F32) for n in range(RING)]
        words = [b[:, :].bitcast(I32) for b in ctxT_buf]
        init_i = words[1][:, 0:TRASH + 1]
        init_t = words[1][:, 512:512 + 2 * (TRASH + 1)].rearrange("p (n c) -> p n c", c=2)
        zeros = words[1][:, 1024:1024 + D].bitcast(F32)
        xg = [ctx_raw[:, a, :] for a in range(AHEAD)]
        y_sb = [ctx_raw[:, AHEAD + u, :] for u in range(2)]
        xgT = [[ctxT_buf[u][:, h * KD * P:(h + 1) * KD * P] for h in range(2)] for u in range(2)]
        sg, hh = (words[u][:, 1024:1024 + HID].bitcast(F32) for u in range(2))
        hhT = [ctxT_buf[0][:, 4096 + h * KH * P:4096 + (h + 1) * KH * P] for h in range(2)]
        bank = [ps(f"bank{n}", [P, 512]) for n in range(8)]
        T_ps, H_ps, O_ps, X_ps, L_ps = bank[0:2], bank[2:4], bank[4:6], bank[6], bank[7]
        T_half = [t[:, :].bitcast(F16)[:, 0:2 * KD * CS].rearrange("p (g c) -> p g c", g=2 * KD)[:, :, 0:CR] for t in T_ps]
        lg_ps, rk_ps = L_ps[0:TT, 0:2 * E], L_ps[0:TT, 64:64 + 2 * E]
        cnt_ps = L_ps[:, 128:128 + E]

        small_loaded = sem("small_loaded")
        consts = sem("consts")
        pool_seq = sem("pool_seq")
        dve_seq = sem("dve_seq")
        tanh_ready = sem("tanh_ready")
        table_ready = sem("table_ready")
        x_loaded = [sem(f"x_loaded{u}") for u in range(2)]
        ctx_loaded = [sem(f"ctx_loaded{q}") for q in range(NQ)]
        ctx_sum_ready, ctx_gsum_ready, ctx_scaled = (sem(n) for n in ("ctx_sum_ready", "ctx_gsum_ready", "ctx_scaled"))
        factors_ready = sem("factors_ready")
        ctx_high, ctx_split = sem("ctx_high"), sem("ctx_split")
        a_high, a_split, xn_high = sem("a_high"), sem("a_split"), sem("xn_high")
        w_loaded, w_sum_ready, w_gsum_ready, w_scaled = (sem(n) for n in ("w_loaded", "w_sum_ready", "w_gsum_ready", "w_scaled"))
        w_high, w_split, cols_ready = (sem(n) for n in ("w_high", "w_split", "cols_ready"))
        ctxT_made, ctxT_ready = sem("ctxT_made"), sem("ctxT_ready")
        h_made, a_ready, attn_part = sem("h_made"), sem("a_ready"), sem("attn_part")
        xn_ready = sem("xn_ready")
        small_made, small_ready = sem("small_made"), sem("small_ready")
        x2_ready, xf_ready = sem("x2_ready"), sem("xf_ready")
        mv1_ready, mv2_ready, rstd1_ready, rstd2_ready = (sem(n) for n in ("mv1_ready", "mv2_ready", "rstd1_ready", "rstd2_ready"))
        logits_made, mask_ready, rank_made, pos_read = (sem(n) for n in ("logits_made", "mask_ready", "rank_made", "pos_read"))
        dl_ready, ex_ready = sem("dl_ready"), sem("ex_ready")
        route_ready = sem("route_ready")
        x2_stored = sem("x2_stored")
        xf_stored = sem("xf_stored")
        routed = [sem(f"routed{u}") for u in range(2)]
        counts_made, map_ready = sem("counts_made"), sem("map_ready")
        phase2 = sem("phase2")
        tables_loaded = sem("tables_loaded")
        meta_loaded = [sem(f"meta_loaded{n}") for n in range(RING)]
        gathered = [sem(f"gathered{a}") for a in range(AHEAD)]
        xgT_made, xgT_ready = sem("xgT_made"), sem("xgT_ready")
        xgT_high, hhT_high = sem("xgT_high"), sem("hhT_high")
        up_made, sg_ready, hh_ready = sem("up_made"), sem("sg_ready"), sem("hh_ready")
        hhT_made, hhT_ready = sem("hhT_made"), sem("hhT_ready")
        y_made, y_ready = sem("y_made"), sem("y_ready")
        added = sem("added")

        def batches(eng, body, seq=None, steps=0, tail=1):
            for i in range(PEEL):
                body(i, i % 2, i // 2)
            pairs = (B - tail - PEEL) // 2
            with eng.Fori(0, pairs) as it:
                if seq:
                    total, seq.base, seq.n = seq.base + seq.n, it * steps + (seq.base + seq.n), 0
                body(it * 2 + PEEL, PEEL % 2, it + PEEL // 2)
                body(it * 2 + (PEEL + 1), (PEEL + 1) % 2, it + (PEEL + 1) // 2)
                if seq:
                    assert seq.n == steps, seq.n
            if seq:
                seq.base, seq.n = total + pairs * steps, 0
            for i in range(B - tail, B):
                body(i, i % 2, i // 2)

        def weight_at(kind, e, part):
            if kind == 2:
                return w2s[:, bass.ds(e * (KH * 2 * D), KH * 2 * D)].rearrange("p (k h n) -> p k h n", k=KH, h=2)[:, :, part, :]
            return w13[:, bass.ds(e * (KD * 4 * HID), KD * 4 * HID)].rearrange("p (k h n) -> p k h n", k=KD, h=2)[:, :, part, kind * HID:(kind + 1) * HID]

        def first_matrix(body, i, u, h):
            if not later(i, 1):
                body(0, 2, E - 1)
            elif u:
                body(h * 3 + 1, 0, h)
            else:
                body(h * 3, 2, h - 1)

        def second_matrix(body, i, u, h):
            if u:
                body(h * 3 + 2, 1, h)

        def late_matrix(body, i, u, h):
            if not u and later(i, 2):
                body(h * 3 - 1, 1, h - 1)

        def blocks(eng, body):
            for b in range(PEEL2):
                body(b, b, 0)
            with eng.Fori(0, (NB - PEEL2) // RING) as it:
                for b in range(PEEL2, PEEL2 + RING):
                    body(it * RING + b, b % RING, it + b // RING)

        block = st.enter_context(nc.Block())

        @block.sync
        def _(sp):
            def load_x(i, u):
                sp.dma_start(x_sb[u][:, :, :], x[bass.ds(i * S, S), :].rearrange("(t p) d -> p t d", p=TT)).then_inc(x_loaded[u], 16)

            def load_ctx(i, q):
                sp.dma_start(ctx_raw[0:CR, 2 * q:2 * q + 2, :],
                             ctx[bass.ds(i * C + 2 * q * CR, 2 * CR), :].rearrange("(c p) d -> p c d", p=CR)).then_inc(ctx_loaded[q], 16)

            def load_weight(n, kind, e):
                if later(n, 1):
                    sp.wait_ge(w_split, n)
                src, rows, k = ((w1, D, KD), (w3, D, KD), (w2, HID, KH))[kind]
                sp.dma_start(w_raw[:, :].rearrange("p (k n) -> p k n", k=k), src[bass.ds(e * rows, rows), :].rearrange("(k p) n -> p k n", p=P)).then_inc(w_loaded, 16)

            for q in range(NQ):
                load_ctx(0, q)
            load_x(0, 0)
            for n, g in enumerate((g_xattn, g_ffn)):
                sp.dma_start(g_raw[:, n:n + 1], g.rearrange("(a n) -> a n", a=1).to_broadcast([P, 1])).then_inc(small_loaded, 16)
            sp.dma_start(gate[:, :, :], gate_w.rearrange("(k p) e -> p k e", p=P)).then_inc(small_loaded, 16)
            load_x(1, 1)
            sp.wait_ge(consts, 1)
            sp.dma_start(table.rearrange("(p n) c -> p n c", p=P), init_t[:, :, :]).then_inc(table_ready, 16)
            sp.dma_start(out[T:T + P, :], zeros).then_inc(table_ready, 16)
            sp.dma_start(xf_dram[T:T + P, :], zeros).then_inc(table_ready, 16)
            for q in range(NQ):
                sp.wait_ge(ctx_split, q + 1)
                load_ctx(1, q)
            first_matrix(load_weight, 0, 0, 0)

            def store_rows(j):
                sp.wait_ge(x2_ready, j * 2 + 2)
                sp.dma_start(out[bass.ds(j * S, S), :].rearrange("(t p) d -> p t d", p=TT), x2[:, :, :]).then_inc(x2_stored, 16)

            def store_norm(j):
                sp.wait_ge(xf_ready, j * 2 + 2)
                sp.dma_start(xf_dram[bass.ds(j * S, S), :].rearrange("(t p) d -> p t d", p=TT), xf[:, :, :]).then_inc(xf_stored, 16)

            def step(i, u, h, load_two=True):
                last = isinstance(i, int) and i == B - 1
                if later(i, 1):
                    store_rows(i - 1)
                    if not last:
                        load_x(i + 1, 1 - u)
                if load_two:
                    for q in range(NQ - 1):
                        sp.wait_ge(ctx_split, i * NQ + (NQ + q + 1))
                        load_ctx(i + 2, q)
                if not u and later(i, 1):
                    first_matrix(load_weight, i, u, h)
                if later(i, 1):
                    store_norm(i - 1)
                if load_two:
                    sp.wait_ge(ctx_split, i * NQ + 2 * NQ)
                    load_ctx(i + 2, NQ - 1)
                second_matrix(load_weight, i, u, h)
                if not u:
                    first_matrix(load_weight, i + 1, 1 - u, h)

            for i in range(PEEL):
                step(i, i % 2, i // 2)
            with sp.Fori(0, (B - 3 - PEEL) // 2) as it:
                step(it * 2 + PEEL, PEEL % 2, it + PEEL // 2)
                step(it * 2 + (PEEL + 1), (PEEL + 1) % 2, it + (PEEL + 1) // 2)
            for i in range(B - 3, B):
                step(i, i % 2, i // 2, i + 2 < B)
            store_rows(B - 1)
            store_norm(B - 1)
            sp.wait_ge(x2_stored, 16 * B)
            sp.wait_ge(xf_stored, 16 * B)
            sp.nop().then_inc(phase2, 1)

            sp.wait_ge(map_ready, 1)
            for v in range(2):
                sp.wait_ge(routed[v], 16 * 2 * TOPK * B // 2)

            def load_meta(b, n):
                if not (isinstance(b, int) and b < RING):
                    sp.wait_ge(added, b * 16 - (RING - 1) * 16)
                row = sp.value_load(bmap[0:1, 1, bass.ds(b, 1)], min_val=0, max_val=TRASH)
                sp.dma_start(meta[n][:, :], table[bass.ds(row * P, P), :]).then_inc(meta_loaded[n], 16)

            for b in range(RING):
                load_meta(b, b)
            with sp.Fori(1, NBM // RING) as it:
                for n in range(RING):
                    load_meta(it * RING + n, n)
            for b in range(NBM - NBM % RING, NBM):
                load_meta(b, b % RING)
            sp.wait_ge(added, 16 * NB)

        @block.gpsimd
        def _(pool):
            seq = Seq(pool, pool_seq)
            g = nc.gpsimd
            seq.done(g.memset(ctx_sum[:, :], 0.0))
            seq.done(g.memset(neg_half[:, :], -0.5))
            seq.done(g.memset(ident[:, :], 0.0))
            seq.hold()
            seq.done(g.affine_select(out=ident[:, :], in_=ident[:, :], compare_op=ALU.not_equal, fill=1.0, base=0, pattern=[[-1, P]], channel_multiplier=1))
            seq.hold()
            seq.done(g.tensor_copy(ident16[:, :], ident[:, :]))
            seq.done(g.iota(init_i, pattern=[[1, TRASH + 1]], base=0, channel_multiplier=TRASH + 1))
            seq.done(g.memset(init_t[:, :, :], 0))
            seq.done(g.memset(zeros, 0.0))
            seq.done(g.memset(lower[:, :], 1.0))
            seq.hold()
            seq.done(g.affine_select(out=lower[:, :], in_=lower[:, :], compare_op=ALU.is_gt, fill=0.0, base=0, pattern=[[1, TT]], channel_multiplier=-1))
            seq.done(g.memset(ones[:, :], 1.0))
            seq.done(g.memset(euler[:, :], float(np.e)))
            seq.done(g.memset(R[:, :, :], 0.0))
            seq.done(g.iota(iota_e[:, :], pattern=[[1, E]], base=0, channel_multiplier=0, allow_small_or_imprecise_dtypes=True))
            seq.done(g.iota(ebase[:, :], pattern=[[T, E]], base=0, channel_multiplier=0, allow_small_or_imprecise_dtypes=True))
            seq.done(g.iota(tok[:, :], pattern=[[TT, 2]], base=0, channel_multiplier=1, allow_small_or_imprecise_dtypes=True))
            seq.done(g.iota(bidx[:, :], pattern=[[1, NBM]], base=0, channel_multiplier=0, allow_small_or_imprecise_dtypes=True))

            def inv_std(mv, at, ready, out_ready, n):
                hold(pool, ready, n)
                seq.done(g.tensor_scalar(ve[:, at:at + 2], mv[:, :, 1], EPS, None, ALU.add))
                seq.hold()
                g.tensor_tensor(rstd[:, at:at + 2], ve[:, at:at + 2], neg_half[:, at:at + 2], ALU.pow).then_inc(out_ready, 1)

            def scale_from(gmax, inv, s):
                seq.done(g.tensor_scalar(exp_i, gmax.bitcast(I32), 0.5 ** (MANT + 1), None, ALU.mult))
                seq.hold()
                seq.done(g.tensor_scalar(exp_f[:, 0:1], exp_i, float(ROOT), float(1 << MANT), ALU.add, ALU.mult))
                seq.hold()
                seq.done(g.tensor_scalar(inv, exp_f[:, 0:1], float((TOP - 1) << MANT), None, ALU.subtract))
                return g.tensor_scalar(s, exp_f[:, 0:1], -1.0, float((2 * BIAS + TOP - 1) << MANT), ALU.mult, ALU.add)

            def context_scale(i, u):
                hold(pool, ctx_sum_ready, i * NQ + NQ)
                g.partition_all_reduce(ctx_gsum[:, :], ctx_sum[:, :], P, bass.bass_isa.ReduceOp.max).then_inc(ctx_gsum_ready, 1)
                hold(pool, ctx_gsum_ready, i + 1)
                seq.done(g.tensor_scalar(ctx_max[:, :], ctx_gsum[:, 0:1], ctx_gsum[:, 1:2], ctx_gsum[:, 2:3], ALU.max, ALU.max))
                seq.hold()
                scale_from(ctx_max[:, :], ctx_inv[u][:, :], ctx_s[u][:, :]).then_inc(ctx_scaled, 1)

            def weight_scale(n, kind, e):
                hold(pool, w_sum_ready, n + 1)
                g.partition_all_reduce(w_gsum[:, :], w_sum[:, :], P, bass.bass_isa.ReduceOp.max).then_inc(w_gsum_ready, 1)
                hold(pool, w_gsum_ready, n + 1)
                scale_from(w_gsum[:, :], w_si[:, :], w_s[:, :]).then_inc(w_scaled, 1)

            def exps(j):
                hold(pool, dl_ready, j + 1)
                g.tensor_tensor(ex[:, :, :].rearrange("p t e -> p (t e)"), euler[:, :], dl[:, :, :].rearrange("p t e -> p (t e)"), ALU.pow).then_inc(ex_ready, 1)

            def send_routes(j, v):
                hold(pool, route_ready, j + 1)
                for t in range(2):
                    for k in range(TOPK):
                        m = t * TOPK + k
                        g.indirect_dma_start(out=table, out_offset=bass.IndirectOffsetOnAxis(ap=pos_i[v][:, m:m + 1], axis=0),
                                             in_=route[v][:, t, k, :], in_offset=None).then_inc(routed[v], 16)

            context_scale(0, 0)
            inv_std(mv1, 0, mv1_ready, rstd1_ready, 1)
            pool.wait_ge(table_ready, 48)
            context_scale(1, 1)

            def step(i, u, h):
                last = isinstance(i, int) and i == B - 1
                if later(i, 1):
                    inv_std(mv2, 2, mv2_ready, rstd2_ready, i)
                if u:
                    first_matrix(weight_scale, i, u, h)
                if not last:
                    inv_std(mv1, 0, mv1_ready, rstd1_ready, i + 2)
                if later(i, 3):
                    send_routes(i - 3, 1 - u)
                if not u:
                    first_matrix(weight_scale, i, u, h)
                if later(i, 2):
                    exps(i - 2)
                if not isinstance(i, int) or i + 2 < B:
                    context_scale(i + 2, u)
                if not last:
                    second_matrix(weight_scale, i, u, h)
                if last:
                    send_routes(i - 2, u)

            batches(pool, step, seq, POOL_STEPS, tail=3)
            inv_std(mv2, 2, mv2_ready, rstd2_ready, B)
            exps(B - 2)
            second_matrix(weight_scale, B - 1, 1, (B - 1) // 2)
            send_routes(B - 2, 0)
            exps(B - 1)
            send_routes(B - 1, 1)

            pool.wait_ge(phase2, 1)
            for v in range(2):
                pool.wait_ge(routed[v], 16 * 2 * TOPK * B // 2)

            def gather(b, n, lap):
                hold(pool, meta_loaded[n], lap * 16 + 16)
                g.indirect_dma_start(out=xg[n % AHEAD], out_offset=None, in_=xf_dram,
                                     in_offset=bass.IndirectOffsetOnAxis(ap=meta[n][:, 0:1], axis=0)).then_inc(gathered[n % AHEAD], 16)

            def scatter(b, n):
                pool.wait_ge(y_ready, b + 1)
                if not (isinstance(b, int) and b == 0):
                    hold(pool, added, b * 16)
                g.indirect_dma_start(out=out, out_offset=bass.IndirectOffsetOnAxis(ap=meta[n][:, 0:1], axis=0),
                                     in_=y_sb[n % 2], in_offset=None, compute_op=ALU.add).then_inc(added, 16)

            for b in range(AHEAD):
                gather(b, b, 0)

            def step2(b, n, lap):
                pool.wait_ge(xgT_made, b + 1)
                gather(b + AHEAD, (n + AHEAD) % RING, lap + (n + AHEAD) // RING)
                if not (isinstance(b, int) and b == 0):
                    scatter(b - 1, (n - 1) % RING)

            blocks(pool, step2)
            scatter(NB - 1, (NB - 1) % RING)
            for a in range(AHEAD):
                pool.wait_ge(gathered[a], 16 * len(range(a, NBM, AHEAD)))
            pool.wait_ge(added, 16 * NB)

        @block.scalar
        def _(act):
            a = nc.scalar

            def ctx_squares(i, q):
                act.wait_ge(ctx_loaded[q], i * 16 + 16)
                if later(i, 1) or q:
                    act.wait_ge(ctx_sum_ready, i * NQ + q)
                a.activation(squares[0][0:CR, :].rearrange("p (c d) -> p c d", c=2), ctx_raw[0:CR, 2 * q:2 * q + 2, :], ACT.Square,
                             accum_out=ctx_sum[0:CR, q:q + 1]).then_inc(ctx_sum_ready, 1)

            def weight_squares(n, kind, e):
                act.wait_ge(w_loaded, n * 16 + 16)
                if later(n, 1):
                    act.wait_ge(w_sum_ready, n)
                a.activation(squares[1][:, :], w_raw[:, :], ACT.Square, accum_out=w_sum[:, :]).then_inc(w_sum_ready, 1)

            def ctx_high_part(i, u, q):
                if q == 0:
                    act.wait_ge(ctx_scaled, i + 1)
                    if later(i, 2):
                        act.wait_ge(attn_part, i * NQ - NQ)
                c = slice(2 * q, 2 * q + 2)
                a.activation(ctx_part[u][0][:, c, :], ctx_raw[0:CR, c, :], ACT.Copy, scale=ctx_s[u][0:CR, :].bitcast(F32)).then_inc(ctx_high, 1)

            def ctxT_out(i, u, c):
                act.wait_ge(ctxT_made, i * NC + c + 1)
                a.activation(ctxT[u][:, :, c * CS:c * CS + CR], T_half[c % 2], ACT.Copy).then_inc(ctxT_ready, 1)

            def gelu(i, u, q):
                n, m = i * NQ + q, (u + q) % 2
                act.wait_ge(h_made, n + 1)
                if q == 0:
                    act.wait_ge(factors_ready, i + 1)
                if later(i, 1) or q == 2:
                    act.wait_ge(a_split, n - 1)
                a.activation(a_f[m][:, :], H_ps[m][0:CR, 0:2 * S], ACT.Gelu_apprx_tanh, scale=h_s[u][0:CR, :]).then_inc(a_ready, 1)
                act.wait_ge(a_ready, n + 1)
                if later(i, 1):
                    act.wait_ge(attn_part, n + 1 - NQ)
                a.activation(a_part[0][:, 2 * q:2 * q + 2, :].rearrange("p c s -> p (c s)"), a_f[m][:, :], ACT.Copy, scale=a_s[u][0:CR, :]).then_inc(a_high, 1)

            def xfT_out(idx, t):
                act.wait_ge(small_made, idx + 1)
                a.activation(xfT[:, t, :, :], X_ps[:, 0:KD * TT].rearrange("p (k r) -> p k r", k=KD), ACT.Copy).then_inc(small_ready, 1)

            def xnT_high(idx, u, t):
                act.wait_ge(small_made, idx + 1)
                a.activation(xnT[u][:, 0, :, t * TT:(t + 1) * TT], X_ps[:, 0:KD * TT].rearrange("p (k r) -> p k r", k=KD), ACT.Copy, scale=2.0 ** X_BITS).then_inc(xn_high, 1)

            def weight_high(n, kind, e):
                hold(act, w_scaled, n + 1)
                a.activation(weight_at(kind, e, 0), w_raw[:, :].rearrange("p (k n) -> p k n", k=(KD, KD, KH)[kind]), ACT.Copy, scale=w_s[:, :].bitcast(F32)).then_inc(w_high, 1)

            act.wait_ge(pool_seq, 1)
            for q in range(NQ):
                ctx_squares(0, q)
            act.wait_ge(small_loaded, 48)
            a.activation(g_tanh[:, :], g_raw[:, :], ACT.Tanh).then_inc(tanh_ready, 1)
            act.wait_ge(tanh_ready, 1)
            a.activation(g_raw[:, 0:1], g_tanh[:, 0:1], ACT.Gelu_apprx_tanh).then_inc(tables_loaded, 1)
            ctx_high_part(0, 0, 0)
            ctx_high_part(0, 0, 1)
            xnT_high(0, 0, 0)
            ctx_high_part(0, 0, 2)
            ctxT_out(0, 0, 0)
            xnT_high(1, 0, 1)
            ctxT_out(0, 0, 1)
            for c in range(2, NC):
                ctxT_out(0, 0, c)
            act.wait_ge(table_ready, 48)
            for q in range(NQ):
                ctx_squares(1, q)

            def step(i, u, h):
                last = isinstance(i, int) and i == B - 1
                w = 1 - u
                two = not isinstance(i, int) or i + 2 < B
                gelu(i, u, 0)
                if not last:
                    ctx_high_part(i + 1, w, 0)
                late_matrix(weight_high, i, u, h)
                if not last:
                    ctx_high_part(i + 1, w, 1)
                gelu(i, u, 1)
                if not last:
                    ctx_high_part(i + 1, w, 2)
                    ctxT_out(i + 1, w, 0)
                    ctxT_out(i + 1, w, 1)
                if u:
                    first_matrix(weight_squares, i, u, h)
                if later(i, 1):
                    xfT_out(i * 4, 0)
                gelu(i, u, 2)
                if u:
                    first_matrix(weight_high, i, u, h)
                if later(i, 1):
                    xfT_out(i * 4 + 1, 1)
                if not last:
                    ctxT_out(i + 1, w, 2)
                if not last:
                    xnT_high(i * 4 + 2, w, 0)
                if not u:
                    first_matrix(weight_squares, i, u, h)
                if not last:
                    ctxT_out(i + 1, w, 3)
                if two:
                    ctx_squares(i + 2, 0)
                if not last:
                    xnT_high(i * 4 + 3, w, 1)
                if not u:
                    first_matrix(weight_high, i, u, h)
                if two:
                    ctx_squares(i + 2, 1)
                if not last:
                    ctxT_out(i + 1, w, 4)
                if two:
                    ctx_squares(i + 2, 2)
                if not last:
                    ctxT_out(i + 1, w, 5)
                second_matrix(weight_squares, i, u, h)

            batches(act, step, tail=3)
            for t in range(2):
                xfT_out((B - 1) * 4 + 2 + t, t)
            late_matrix(weight_high, B, 0, B // 2)

            a.activation(g_raw[:, 0:1], g_raw[:, 1:2], ACT.Silu).then_inc(tables_loaded, 1)

            def rows_high(b, u):
                act.wait_ge(xgT_made, b + 1)
                a.activation(xgT[u][0], T_ps[u][:, :], ACT.Copy, scale=2.0 ** X_BITS).then_inc(xgT_high, 1)

            def hid_high(b):
                act.wait_ge(hhT_made, b + 1)
                a.activation(hhT[0], bank[6][:, 0:KH * P], ACT.Copy).then_inc(hhT_high, 1)

            rows_high(0, 0)

            def y_out(b, u):
                act.wait_ge(y_made, b + 1)
                if not (isinstance(b, int) and b < 2):
                    act.wait_ge(added, (b - 1) * 16)
                a.activation(y_sb[u], O_ps[u][:, :], ACT.Copy, scale=cols[u][:, 1:2]).then_inc(y_ready, 1)

            def step2(b, n, lap):
                first_, u = isinstance(b, int) and b == 0, n % 2
                if not first_:
                    hid_high(b - 1)
                rows_high(b + 1, 1 - u)
                act.wait_ge(cols_ready, b + 1)
                act.wait_ge(up_made, b + 1)
                if not first_:
                    act.wait_ge(hh_ready, b)
                a.activation(sg, H_ps[u][:, 0:HID], ACT.Silu, scale=cols[u][:, 0:1]).then_inc(sg_ready, 1)
                if not first_:
                    y_out(b - 1, 1 - u)

            blocks(act, step2)
            hid_high(NB - 1)
            y_out(NB - 1, (NB - 1) % 2)

        @block.vector
        def _(dve):
            v = nc.vector
            seq = Seq(dve, dve_seq)

            def start_table():
                dve.wait_ge(pool_seq, POOL_START)
                seq.done(v.tensor_scalar(init_i, init_i, P - 1, None, ALU.bitwise_and))
                seq.settle()
                v.tensor_scalar(init_t[:, :, 0], init_i, float(T), None, ALU.add).then_inc(consts, 1)

            def norm_stats(src, mv, ready):
                for t in range(2):
                    seq.done(v.bn_stats(stats[:, t, :], src[:, t, :]))
                seq.hold()
                for t in range(2):
                    last = v.bn_aggr(mv[:, t, :], stats[:, t, :])
                    if t == 0:
                        seq.done(last)
                last.then_inc(ready, 1)

            def context_factors(i, u):
                dve.wait_ge(ctx_scaled, i + 1)
                if later(i, 2):
                    dve.wait_ge(x2_ready, i * 2 - 2)
                s, inv = ctx_s[u][:, :].bitcast(F32), ctx_inv[u][:, :].bitcast(F32)
                seq.done(v.tensor_scalar(a_s[u][:, :], s, 2.0 ** A_BITS, None, ALU.mult))
                seq.done(v.tensor_scalar(o_s[u][:, :], inv, inv, tanh_a[:, :], ALU.mult, ALU.mult))
                v.tensor_scalar(h_s[u][:, :], inv, 2.0 ** -X_BITS, None, ALU.mult).then_inc(factors_ready, 1)

            def context_low(i, u, q):
                dve.wait_ge(ctx_high, i * NQ + q + 1)
                c = slice(2 * q, 2 * q + 2)
                v.scalar_tensor_tensor(ctx_part[u][1][:, c, :], ctx_raw[0:CR, c, :], ctx_s[u][0:CR, :].bitcast(F32), ctx_part[u][0][:, c, :],
                                       ALU.mult, ALU.subtract).then_inc(ctx_split, 1)

            def a_low(i, u, q):
                m = (u + q) % 2
                dve.wait_ge(a_high, i * NQ + q + 1)
                c = slice(2 * q, 2 * q + 2)
                high, low = (a_part[h][:, c, :].rearrange("p c s -> p (c s)") for h in range(2))
                v.scalar_tensor_tensor(low, a_f[m][:, :], a_s[u][0:CR, :], high, ALU.mult, ALU.subtract).then_inc(a_split, 1)

            def stats1(i, u, n_x):
                dve.wait_ge(x_loaded[u], n_x)
                norm_stats(x_sb[u], mv1, mv1_ready)

            def norm1(i, u):
                dve.wait_ge(mv1_ready, i + 1)
                dve.wait_ge(rstd1_ready, i + 1)
                if later(i, 1):
                    dve.wait_ge(small_made, i * 4 - 4 if later(i, 2) else 2)
                for t in range(2):
                    v.tensor_scalar(xn[:, t, :], x_sb[u][:, t, :], mv1[:, t, 0:1], rstd[:, t:t + 1], ALU.subtract, ALU.mult).then_inc(xn_ready, 1)

            def xnT_low(i, idx, u, t):
                dve.wait_ge(xn_high, i * 2 + t + 1)
                src = X_ps[:, 0:KD * TT].rearrange("p (k r) -> p k r", k=KD)
                high, low = (xnT[u][:, h, :, t * TT:(t + 1) * TT] for h in range(2))
                v.scalar_tensor_tensor(low, src, 2.0 ** X_BITS, high, ALU.mult, ALU.subtract).then_inc(small_ready, 1)

            def residual(j, u):
                dve.wait_ge(attn_part, j * NQ + NQ)
                if later(j, 1):
                    dve.wait_ge(x2_stored, j * 16)
                for t in range(2):
                    v.scalar_tensor_tensor(x2[:, t, :], O_ps[t][0:TT, :], o_s[u][0:TT, :], x_sb[u][:, t, :], ALU.mult, ALU.add).then_inc(x2_ready, 1)

            def stats2(j):
                dve.wait_ge(x2_ready, j * 2 + 2)
                norm_stats(x2, mv2, mv2_ready)

            def norm2(j):
                dve.wait_ge(mv2_ready, j + 1)
                dve.wait_ge(rstd2_ready, j + 1)
                if later(j, 1):
                    dve.wait_ge(xf_stored, j * 16)
                    dve.wait_ge(small_made, j * 4 + 2)
                for t in range(2):
                    v.tensor_scalar(xf[:, t, :], x2[:, t, :], mv2[:, t, 0:1], rstd[:, 2 + t:3 + t], ALU.subtract, ALU.mult).then_inc(xf_ready, 1)

            def route_top(j):
                dve.wait_ge(logits_made, j + 1)
                seq.done(v.tensor_copy(lg[:, :, :].rearrange("p t e -> p (t e)"), lg_ps))
                seq.hold()
                for t in range(2):
                    seq.done(v.max(mx[:, t, :], lg[:, t, :]))
                seq.hold()
                for t in range(2):
                    seq.done(v.max_index(ix[:, t, :], mx[:, t, :], lg[:, t, :]))
                for t in range(2):
                    ins = v.tensor_scalar(dl[:, t, :], mx[:, t, :], mx[:, t, 0:1], None, ALU.subtract)
                    if t == 0:
                        seq.done(ins)
                ins.then_inc(dl_ready, 1)
                seq.settle()
                seq.done(v.tensor_copy(ixf[:, :, :], ix[:, :, 0:TOPK]))
                seq.settle()
                for t in range(2):
                    for k in range(TOPK):
                        seq.done(v.tensor_scalar(oh[:, t, k, :], iota_e[:, :], ixf[:, t, k:k + 1], None, ALU.is_equal))
                seq.settle()
                seq.done(v.tensor_tensor(M[:, :, :], oh[:, :, 0, :], oh[:, :, 1, :], ALU.add))
                seq.settle()
                v.tensor_tensor(R[:, 1, :], R[:, 0, :], M[:, 0, :], ALU.add).then_inc(mask_ready, 1)

            def route_scores(j, u):
                dve.wait_ge(ex_ready, j + 1)
                seq.done(v.reduce_sum(sm[:, :], ex[:, :, :], AX.X))
                seq.settle()
                seq.done(v.reciprocal(rs[:, :], sm[:, :]))
                for k in range(TOPK):
                    seq.done(v.tensor_copy(route[u][:, :, k, 0], tok[:, :]))
                seq.settle()
                for t in range(2):
                    seq.done(v.tensor_scalar(route[u][:, t, :, 1].bitcast(F32), ex[:, t, 0:TOPK], rs[:, t:t + 1], None, ALU.mult))
                seq.settle()
                v.tensor_scalar(tok[:, :], tok[:, :], float(S), None, ALU.add).then_inc(route_ready, 1)

            def route_pos(j, u, hj):
                if later(j, 2):
                    dve.wait_ge(routed[u], hj * (16 * 2 * TOPK))
                dve.wait_ge(rank_made, j + 1)
                seq.done(v.tensor_tensor(R[:, 0, :], R[:, 1, :], M[:, 1, :], ALU.add))
                for t in range(2):
                    ins = v.tensor_tensor(pos_e[:, t, :], rk_ps[:, t * E:(t + 1) * E], ebase[:, :], ALU.add)
                    if t == 0:
                        seq.done(ins)
                ins.then_inc(pos_read, 1)
                dve.wait_ge(pos_read, j + 1)
                seq.settle()
                for k in range(TOPK):
                    seq.done(v.tensor_tensor(pos_o[:, :, k, :], pos_e[:, :, :], oh[:, :, k, :], ALU.mult))
                seq.settle()
                seq.done(v.reduce_sum(pos_f[:, :], pos_o[:, :, :, :].rearrange("p t k e -> p (t k) e"), AX.X))
                seq.settle()
                seq.done(v.tensor_copy(pos_i[u][:, :], pos_f[:, :]))

            def weight_low(n, kind, e):
                dve.wait_ge(w_high, n + 1)
                seq.done(v.tensor_copy(w_inv[:, kind, bass.ds(e, 1)], w_si[:, :]))
                if kind == 0:
                    seq.done(v.tensor_copy(w1_s[:, bass.ds(e, 1)], w_s[:, :].bitcast(F32)))
                part = [weight_at(kind, e, h) for h in range(2)]
                v.scalar_tensor_tensor(part[1], w_raw[:, :].rearrange("p (k n) -> p k n", k=(KD, KD, KH)[kind]), w_s[:, :].bitcast(F32), part[0],
                                       ALU.mult, ALU.subtract).then_inc(w_split, 1)

            stats1(0, 0, 16)
            start_table()
            dve.wait_ge(tanh_ready, 1)
            seq.done(v.tensor_scalar(tanh_a[:, :], g_tanh[:, 0:1], 2.0 ** -A_BITS, None, ALU.mult))
            seq.settle()
            context_factors(0, 0)
            context_low(0, 0, 0)
            norm1(0, 0)
            context_low(0, 0, 1)
            xnT_low(0, 0, 0, 0)
            context_low(0, 0, 2)
            xnT_low(0, 1, 0, 1)

            def step(i, u, h):
                last = isinstance(i, int) and i == B - 1
                j, w = i - 1, 1 - u
                if later(i, 1):
                    residual(j, w)
                if not u and later(i, 1):
                    stats2(j)
                a_low(i, u, 0)
                if u:
                    stats2(j)
                if not last:
                    context_low(i + 1, w, 0)
                if not last:
                    context_factors(i + 1, w)
                if later(i, 3):
                    route_scores(i - 3, w)
                if not last:
                    context_low(i + 1, w, 1)
                late_matrix(weight_low, i, u, h)
                a_low(i, u, 1)
                if later(i, 1):
                    norm2(j)
                if last:
                    route_top(i - 2)
                if not last:
                    stats1(i + 1, w, (h + u) * 16 + 16)
                    context_low(i + 1, w, 2)
                a_low(i, u, 2)
                if not last:
                    norm1(i + 1, w)
                if u:
                    first_matrix(weight_low, i, u, h)
                if not last:
                    xnT_low(i + 1, i * 4 + 2, w, 0)
                if later(i, 2) and not last:
                    route_top(i - 2)
                if not last:
                    xnT_low(i + 1, i * 4 + 3, w, 1)
                if not u:
                    first_matrix(weight_low, i, u, h)
                if later(i, 2):
                    route_pos(i - 2, u, h - 1)
                if last:
                    route_scores(i - 2, u)

            batches(dve, step, seq, DVE_STEPS)
            residual(B - 1, 1)
            stats2(B - 1)
            route_top(B - 2)
            norm2(B - 1)
            route_pos(B - 2, 0, (B - 2) // 2)
            route_scores(B - 2, 0)
            late_matrix(weight_low, B, 0, B // 2)
            route_top(B - 1)
            route_pos(B - 1, 1, (B - 1) // 2)

            def one(ins):
                seq.done(ins)
                seq.settle()

            seq.done(v.memset(sums[:, :, :], 0.0))
            dve.wait_ge(counts_made, 1)
            one(v.tensor_scalar(cnt_i, cnt_ps[0:1, :], float(P - 1), None, ALU.add))
            one(v.tensor_scalar(cnt_i, cnt_i, P.bit_length() - 1, None, ALU.logical_shift_right))
            nblk, first = sums[:, 0, E // 2 + 1:], sums[:, 3, E // 2:]
            seq.done(v.tensor_copy(nblk, cnt_i))
            seq.settle()
            seq.done(v.tensor_scalar(gap, nblk, -1.0, float(EB), ALU.mult, ALU.add))
            for n in range(3):
                one(v.tensor_tensor(sums[:, n + 1, E // 2:], sums[:, n, E // 2:], sums[:, n, E // 2 - 2 ** n:-2 ** n], ALU.add))
            route_scores(B - 1, 1)
            spread = [1, E - 1, NBM]
            one(v.tensor_tensor(is_from, bidx[:, :].rearrange("p (o b) -> p o b", o=1).to_broadcast(spread),
                                first[:, 1:E].rearrange("p (e o) -> p e o", o=1).to_broadcast(spread), ALU.is_ge))
            seq.done(v.reduce_sum(m_e, is_from.rearrange("p e b -> p b e"), AX.X))
            one(v.tensor_tensor(skipped, is_from, gap[:, 0:E - 1].rearrange("p (e o) -> p e o", o=1).to_broadcast(spread), ALU.mult))
            one(v.reduce_sum(m_r, skipped.rearrange("p e b -> p b e"), AX.X))
            seq.done(v.tensor_scalar(m_t, bidx[:, :], first[:, E:E + 1], None, ALU.is_lt))
            one(v.scalar_tensor_tensor(m_r, m_r, float(-TRASH), bidx[:, :], ALU.add, ALU.add))
            one(v.tensor_tensor(m_r, m_r, m_t, ALU.mult))
            seq.done(v.tensor_copy(bmap[:, 0, :], m_e))
            one(v.tensor_scalar(bmap[:, 1, :], m_r, float(TRASH), None, ALU.add))
            v.engine_nop().then_inc(map_ready, 1)

            seq.settle()
            inv = w_inv[:, :, :].bitcast(F32)
            Qe = Q[:, :].rearrange("p (e c) -> p e c", c=3)
            seq.done(v.tensor_scalar(Qe[:, :, 0], inv[:, 0, :], 2.0 ** -X_BITS, None, ALU.mult))
            seq.done(v.tensor_scalar(Qe[:, :, 2], w1_s[:, :], 2.0 ** (HID_BITS - X_BITS), None, ALU.mult))
            one(v.scalar_tensor_tensor(q_tmp[:, 0, :], inv[:, 0, :], 2.0 ** -HID_BITS, inv[:, 1, :], ALU.mult, ALU.mult))
            one(v.tensor_tensor(q_tmp[:, 1, :], q_tmp[:, 0, :], inv[:, 2, :], ALU.mult))
            one(v.tensor_scalar(Qe[:, :, 1], q_tmp[:, 1, :], g_tanh[:, 1:2], None, ALU.mult))

            def rows_low(b, u):
                dve.wait_ge(xgT_high, b + 1)
                v.scalar_tensor_tensor(xgT[u][1], T_ps[u][:, :], 2.0 ** X_BITS, xgT[u][0], ALU.mult, ALU.subtract).then_inc(xgT_ready, 1)

            def hid_low(b):
                dve.wait_ge(hhT_high, b + 1)
                v.tensor_tensor(hhT[1], bank[6][:, 0:KH * P], hhT[0], ALU.subtract).then_inc(hhT_ready, 1)

            rows_low(0, 0)

            def step2(b, n, lap):
                u, first_ = n % 2, isinstance(b, int) and b == 0
                if not (isinstance(b, int) and b < 2):
                    dve.wait_ge(y_ready, b - 1)
                dve.wait_ge(meta_loaded[n], lap * 16 + 16)
                e = dve.value_load(bmap[0:1, 0, bass.ds(b, 1)], min_val=0, max_val=E - 1)
                v.tensor_scalar(cols[u][:, 0:2], Q[:, bass.ds(e * 3, 2)], score[n], None, ALU.mult)
                v.tensor_copy(cols[u][:, 2:3], Q[:, bass.ds(e * 3 + 2, 1)]).then_inc(cols_ready, 1)
                if not first_:
                    hid_low(b - 1)
                rows_low(b + 1, 1 - u)
                dve.wait_ge(cols_ready, b + 1)
                dve.wait_ge(sg_ready, b + 1)
                if not first_:
                    dve.wait_ge(hhT_made, b)
                v.scalar_tensor_tensor(hh, H_ps[u][:, HID:2 * HID], cols[u][:, 2:3], sg, ALU.mult, ALU.mult).then_inc(hh_ready, 1)

            blocks(dve, step2)
            hid_low(NB - 1)

        @block.tensor
        def _(pe):
            t_ = nc.tensor
            pe.wait_ge(pool_seq, POOL_IDENT)

            def trans_ctx(i, u, c):
                n = i * NC + c
                pe.wait_ge(ctx_split, i * NQ + c // 2 + 1)
                if later(i, 1) or c >= 2:
                    pe.wait_ge(ctxT_ready, n - 1)
                for h in range(2):
                    for k in range(KD):
                        ins = t_.transpose(T_half[c % 2][:, h * KD + k, :], ctx_part[u][h][:, c, k * P:(k + 1) * P], ident16[0:CR, 0:CR])
                ins.then_inc(ctxT_made, 1)

            def small_trans(idx, src):
                if later(idx, 1):
                    pe.wait_ge(small_ready, idx)
                for k in range(KD):
                    ins = t_.transpose(X_ps[:, k * TT:(k + 1) * TT], src[:, k * P:(k + 1) * P], ident[0:TT, 0:TT])
                ins.then_inc(small_made, 1)

            def scores(i, u, q):
                n, m = i * NQ + q, (u + q) % 2
                if q == 0:
                    pe.wait_ge(small_ready, i * 4 if later(i, 1) else 2)
                pe.wait_ge(ctxT_ready, i * NC + 2 * q + 2)
                if later(i, 1) or q == 2:
                    pe.wait_ge(a_ready, n - 1)
                for c in (2 * q, 2 * q + 1):
                    dst = H_ps[m][0:CR, (c % 2) * S:(c % 2 + 1) * S]
                    for j, (k, (hc, hx)) in enumerate((k, part) for k in range(KD) for part in PARTS):
                        ins = t_.matmul(dst, ctxT[u][:, hc * KD + k, c * CS:c * CS + CR], xnT[u][:, hx, k, :], start=j == 0, stop=j == KD * len(PARTS) - 1)
                ins.then_inc(h_made, 1)

            def attend(i, u, q, halves=(0, 1)):
                if 0 in halves:
                    pe.wait_ge(a_split, i * NQ + q + 1)
                    if q == 0 and later(i, 1):
                        pe.wait_ge(x2_ready, i * 2)
                for c in (2 * q + half for half in halves):
                    for t in range(2):
                        for ha, hc in PARTS:
                            ins = t_.matmul(O_ps[t][0:TT, :], a_part[ha][:, c, t * TT:(t + 1) * TT], ctx_part[u][hc][:, c, :],
                                            start=c == 0 and (ha, hc) == PARTS[0], stop=c == NC - 1 and (ha, hc) == PARTS[-1])
                if 1 in halves:
                    ins.then_inc(attn_part, 1)

            def rows_norm2(j, idx, t):
                pe.wait_ge(xf_ready, j * 2 + t + 1)
                small_trans(idx, xf[:, t, :])

            def rows_norm1(i, idx, t):
                pe.wait_ge(xn_ready, i * 2 + t + 1)
                small_trans(idx, xn[:, t, :])

            def logits(j):
                pe.wait_ge(small_ready, 4 * B if isinstance(j, int) and j == B - 1 else j * 4 + 6)
                if later(j, 1):
                    pe.wait_ge(pos_read, j)
                for t in range(2):
                    for k in range(KD):
                        ins = t_.matmul(lg_ps[:, t * E:(t + 1) * E], xfT[:, t, k, :], gate[:, k, :], start=k == 0, stop=k == KD - 1)
                ins.then_inc(logits_made, 1)

            def rank(j):
                pe.wait_ge(mask_ready, j + 1)
                if later(j, 1):
                    pe.wait_ge(pos_read, j)
                t_.matmul(rk_ps, lower[:, :], M[:, :, :].rearrange("p t e -> p (t e)"), start=True, stop=False)
                t_.matmul(rk_ps, ones[:, 0:TT], R[:, :, :].rearrange("p t e -> p (t e)"), start=False, stop=True).then_inc(rank_made, 1)

            pe.wait_ge(small_loaded, 48)
            for t in range(2):
                rows_norm1(0, t, t)
                trans_ctx(0, 0, t)
            for c in range(2, NC):
                trans_ctx(0, 0, c)
            pe.wait_ge(pool_seq, POOL_START)

            def step(i, u, h):
                last = isinstance(i, int) and i == B - 1
                w = 1 - u
                scores(i, u, 0)
                scores(i, u, 1)
                if later(i, 2):
                    logits(i - 2)
                attend(i, u, 0)
                if not last:
                    trans_ctx(i + 1, w, 0)
                    trans_ctx(i + 1, w, 1)
                scores(i, u, 2)
                if later(i, 1):
                    rows_norm2(i - 1, i * 4, 0)
                attend(i, u, 1)
                if last:
                    rank(i - 2)
                if later(i, 1):
                    rows_norm2(i - 1, i * 4 + 1, 1)
                if not last:
                    trans_ctx(i + 1, w, 2)
                    trans_ctx(i + 1, w, 3)
                if not last:
                    rows_norm1(i + 1, i * 4 + 2, 0)
                attend(i, u, 2, (0,))
                if not last:
                    rows_norm1(i + 1, i * 4 + 3, 1)
                attend(i, u, 2, (1,))
                if not last:
                    trans_ctx(i + 1, w, 4)
                    trans_ctx(i + 1, w, 5)
                if later(i, 2) and not last:
                    rank(i - 2)

            batches(pe, step)
            logits(B - 2)
            rank(B - 2)
            for t in range(2):
                rows_norm2(B - 1, (B - 1) * 4 + 2 + t, t)
            logits(B - 1)
            rank(B - 1)
            pe.wait_ge(pos_read, B)
            t_.matmul(cnt_ps, ones[:, :], R[:, 0, :], start=True, stop=True).then_inc(counts_made, 1)

            pe.wait_ge(w_split, 3 * E)
            pe.wait_ge(map_ready, 1)

            def trans_rows(b, n, lap):
                u, a = n % 2, n % AHEAD
                pe.wait_ge(gathered[a], lap * (16 * RING // AHEAD) + 16 * (n // AHEAD + 1))
                if not isinstance(b, int) or b >= 2:
                    pe.wait_ge(xgT_ready, b - 1)
                for k in range(KD):
                    ins = t_.transpose(T_ps[u][:, k * P:(k + 1) * P], xg[a][:, k * P:(k + 1) * P], ident[:, :])
                ins.then_inc(xgT_made, 1)

            def trans_hid(b):
                pe.wait_ge(hh_ready, b + 1)
                if not (isinstance(b, int) and b == 0):
                    pe.wait_ge(hhT_ready, b)
                for k in range(KH):
                    ins = t_.transpose(bank[6][:, k * P:(k + 1) * P], hh[:, k * P:(k + 1) * P], ident[:, :])
                ins.then_inc(hhT_made, 1)

            def up(b, u, e, first2):
                pe.wait_ge(xgT_ready, b + 1)
                if not first2:
                    pe.wait_ge(hh_ready, b - 1)
                for m, (k, part) in enumerate((k, part) for k in range(KD) for part in PARTS):
                    rows = xgT[u][part[0]][:, k * P:(k + 1) * P]
                    w = w13[:, bass.ds(e * (KD * 4 * HID) + (2 * k + part[1]) * 2 * HID, 2 * HID)]
                    ins = t_.matmul(H_ps[u][:, :], rows, w, start=m == 0, stop=m == KD * len(PARTS) - 1)
                ins.then_inc(up_made, 1)

            def down(b, u, e, first2):
                pe.wait_ge(hhT_ready, b + 1)
                if not first2:
                    pe.wait_ge(y_ready, b - 1)
                for m, (k, part) in enumerate((k, part) for k in range(KH) for part in PARTS):
                    rows = hhT[part[0]][:, k * P:(k + 1) * P]
                    ins = t_.matmul(O_ps[u][:, :], rows, w2s[:, bass.ds(e * (KH * 2 * D) + (2 * k + part[1]) * D, D)], start=m == 0, stop=m == KH * len(PARTS) - 1)
                ins.then_inc(y_made, 1)

            def expert(b):
                return pe.value_load(bmap[0:1, 0, bass.ds(b, 1)], min_val=0, max_val=E - 1)

            trans_rows(0, 0, 0)

            loaded = [None]

            def step2(b, n, lap):
                u = n % 2
                if isinstance(b, int) and b == 0:
                    trans_rows(1, 1, 0)
                    loaded[0] = expert(0)
                    up(0, 0, loaded[0], True)
                    return
                small = isinstance(b, int)
                e_up, e_down = expert(b), expert(b - 1) if n == PEEL2 % RING and not small else loaded[0]
                loaded[0] = e_up
                trans_rows(b + 1, n + 1, lap)
                trans_hid(b - 1)
                up(b, u, e_up, small and b < 2)
                down(b - 1, 1 - u, e_down, small and b - 1 < 2)

            blocks(pe, step2)
            trans_hid(NB - 1)
            down(NB - 1, (NB - 1) % 2, expert(NB - 1), False)


DVE_STEPS = 68
POOL_STEPS = 21
POOL_IDENT = 5
POOL_START = 17


_INS = ['x', 'ctx_1024', 'g_xattn', 'g_ffn', 'L0_ffn_gate_w', 'L0_ffn_w1', 'L0_ffn_w2', 'L0_ffn_w3']


def kernel(**inputs):
    import concourse.bacc as _bacc
    from concourse.bass_utils import run_bass_kernel_spmd as _run

    nc = _bacc.Bacc("TRN2", target_bir_lowering=False, num_devices=1)
    arrays, args = {}, []
    for name in _INS:
        a = np.ascontiguousarray(inputs[name])
        if a.ndim == 3:
            a = a.reshape(-1, a.shape[-1])
        arrays[f"in_{name}"] = a
        args.append(nc.dram_tensor(f"in_{name}", a.shape, mybir.dt.from_np(a.dtype), kind="ExternalInput").ap())
    args.append(nc.dram_tensor("out_rows", (T + P, D), F32, kind="ExternalOutput").ap())
    build(nc, *args)
    r = _run(nc, [arrays], core_ids=[0])
    return r.results[0]["out_rows"][:T].reshape(B, S, D)
```
